# Optimizing a Trainium2 kernel written in Bass

```python
import numpy as np
import jax
import jax.numpy as jnp

def _softmax(x, axis=-1):
    return jax.nn.softmax(x, axis=axis)

def _gelu(x):
    return jax.nn.gelu(x, approximate=True)

def _silu(x):
    return jax.nn.silu(x)

def _sigmoid(x):
    return jax.nn.sigmoid(x)

def _layernorm(x, axis=-1, eps=1e-05):
    m = jnp.mean(x, axis=axis, keepdims=True)
    v = jnp.var(x, axis=axis, keepdims=True)
    return (x - m) / jnp.sqrt(v + eps)

def _scatter_add(tgt, idx, src, axis=0):
    return tgt.at[idx].add(src)

def _segment_sum(src, seg, n):
    return jax.ops.segment_sum(src, seg, n)
kernel_name = 'mk_gps_d1_gnn_r32_bc4a75'

def setup_inputs(seed: int=0):
    np.random.seed(seed)
    _w = jnp.asarray

    def _rec_inputs():
        import jax
        import jax.numpy as jnp
        _gk = jax.random.key(seed)
        x = -0.0005963 + 1.001 * jax.random.normal(jax.random.fold_in(_gk, 1), (96, 1024), jnp.float32)
        src = jax.random.randint(jax.random.fold_in(_gk, 2), (3072,), 0, 96, jnp.int32)
        dst = jnp.minimum((96 * jax.random.uniform(jax.random.fold_in(_gk, 3), (3072,)) ** 2.0).astype(jnp.int32), 3071)
        _o = jnp.argsort(dst, stable=True)
        src = src[_o]
        dst = dst[_o]
        edge_type_5 = jax.random.randint(jax.random.fold_in(_gk, 12), (3072,), 0, 5, jnp.int32)
        return (x, src, dst, edge_type_5)
    x, src, dst, edge_type_5 = _rec_inputs()

    def _L0_gnn_setup():
        import jax, jax.numpy as jnp
        import numpy as np
        N = 96
        E = 3072
        IN_F = 1024
        OUT_F = 1024
        H = 16
        D = OUT_F // H
        NUM_ETYPES = 4

        def _build_mask(edge_index, edge_type, edge_type_weights, dtype):
            src, dst = (edge_index[0], edge_index[1])
            w = jax.nn.softplus(edge_type_weights)
            mask = jnp.full((N, N), -jnp.inf, dtype=dtype)
            mask = mask.at[src, dst].set(w[edge_type - 1])
            diag = jnp.diagonal(mask)
            idx = jnp.arange(N)
            mask = mask.at[idx, idx].set(jnp.where(jnp.isneginf(diag), w[3], diag))
            return mask
        key = jax.random.key(seed)
        ks = jax.random.split(key, 20)
        p = lambda k, shape: jax.random.normal(k, shape, dtype=jnp.float32) * 0.02
        return {'x': jax.random.normal(ks[0], (N, IN_F), dtype=jnp.float32), 'edge_index': jax.random.randint(ks[1], (2, E), 0, N), 'edge_type': jax.random.randint(ks[2], (E,), 1, NUM_ETYPES + 1), 'edge_type_weights': jnp.ones((NUM_ETYPES,), jnp.float32) + 0.1 * jax.random.normal(ks[3], (NUM_ETYPES,), dtype=jnp.float32), 'wq': p(ks[4], (OUT_F, IN_F)), 'bq': p(ks[5], (OUT_F,)), 'wk': p(ks[6], (OUT_F, IN_F)), 'bk': p(ks[7], (OUT_F,)), 'wv': p(ks[8], (OUT_F, IN_F)), 'bv': p(ks[9], (OUT_F,)), 'wiq': p(ks[10], (OUT_F, OUT_F)), 'biq': p(ks[11], (OUT_F,)), 'wik': p(ks[12], (OUT_F, OUT_F)), 'bik': p(ks[13], (OUT_F,)), 'wiv': p(ks[14], (OUT_F, OUT_F)), 'biv': p(ks[15], (OUT_F,)), 'wo': p(ks[16], (OUT_F, OUT_F)), 'bo': p(ks[17], (OUT_F,))}
    _L0_gnn_all = _L0_gnn_setup()
    _L0_gnn_in = {k: v for k, v in _L0_gnn_all.items() if k in ('edge_type_weights', 'wq', 'bq', 'wk', 'bk', 'wv', 'bv', 'wiq', 'biq', 'wik', 'bik', 'wiv', 'biv', 'wo', 'bo')}
    del _L0_gnn_all

    def _L0_mix_setup():
        import jax, jax.numpy as jnp
        import numpy as np
        N_HEAD = 16
        D_HEAD = 64
        D_MODEL = 1024
        N_ROLL = 3
        SCALE = 1.0 / D_HEAD ** 0.5
        EPS = 1e-05

        def mul_roll_repeat(x, n_roll):
            return jnp.concatenate([x * jnp.roll(x, i, axis=-1) for i in range(1, n_roll + 1)], axis=-1)

        def dpfp(x):
            x2 = jnp.concatenate([jax.nn.relu(x), jax.nn.relu(-x)], axis=-1)
            return mul_roll_repeat(x2, N_ROLL)

        def layer_norm(x, gamma, beta):
            mu = jnp.mean(x, axis=-1, keepdims=True)
            var = jnp.var(x, axis=-1, keepdims=True)
            return (x - mu) * jax.lax.rsqrt(var + 1e-05) * gamma + beta
        key = jax.random.key(seed)
        ks = jax.random.split(key, 4)
        S, B = (64, 2)
        h = jax.random.normal(ks[0], (S, B, D_MODEL), dtype=jnp.float32)
        Wq = jax.random.normal(ks[1], (D_MODEL, N_HEAD * D_HEAD), dtype=jnp.float32) * 0.02
        Wkv = jax.random.normal(ks[2], (D_MODEL, 2 * N_HEAD * D_HEAD), dtype=jnp.float32) * 0.02
        Wo = jax.random.normal(ks[3], (N_HEAD * D_HEAD, D_MODEL), dtype=jnp.float32) * 0.02
        ln_gamma = jnp.ones((D_MODEL,), dtype=jnp.float32)
        ln_beta = jnp.zeros((D_MODEL,), dtype=jnp.float32)
        return {'h': h, 'Wq': Wq, 'Wkv': Wkv, 'Wo': Wo, 'ln_gamma': ln_gamma, 'ln_beta': ln_beta}
    _L0_mix_all = _L0_mix_setup()
    _L0_mix_in = {k: v for k, v in _L0_mix_all.items() if k in ('Wq', 'Wkv', 'Wo', 'ln_gamma', 'ln_beta')}
    del _L0_mix_all

    def _L0_ffn_setup():
        import jax, jax.numpy as jnp
        import numpy as np
        BS, SLEN, DIM = (1, 64, 1024)
        NUM_EXPERTS, TOP_K = (8, 2)
        HID = 1408

        def _masked_grouped_mm(x, w, onehot):
            g = jnp.einsum('tk,gnk->tgn', x, w, preferred_element_type=jnp.float32)
            return jnp.einsum('tgn,tg->tn', g, onehot)

        def moe_forward(x, gate_w, expert_bias, w_up, w_down, shared_w_up, shared_w_down):
            bs, slen, dim = x.shape
            xf = x.reshape(-1, dim)
            scores = jax.nn.sigmoid((xf @ gate_w.T).astype(jnp.float32))
            biased = scores + expert_bias
            _, sel = jax.lax.top_k(biased, TOP_K)
            top_scores = jnp.take_along_axis(scores, sel, axis=-1)
            flat_sel = sel.reshape(-1)
            counts = jnp.bincount(flat_sel, length=NUM_EXPERTS)
            order = jnp.argsort(flat_sel, stable=True)
            scores_sorted = top_scores.reshape(-1)[order]
            token_ids = order // TOP_K
            routed_in = (xf[token_ids] * scores_sorted[:, None]).astype(x.dtype)
            seg = jnp.repeat(jnp.arange(NUM_EXPERTS), counts, total_repeat_length=flat_sel.shape[0])
            onehot = jax.nn.one_hot(seg, NUM_EXPERTS, dtype=jnp.float32)
            h = _masked_grouped_mm(routed_in.astype(jnp.bfloat16), w_up.astype(jnp.bfloat16), onehot)
            h = jnp.square(jax.nn.relu(h.astype(jnp.bfloat16)))
            routed_out = _masked_grouped_mm(h.astype(jnp.bfloat16), w_down.astype(jnp.bfloat16), onehot)
            routed_out = routed_out.astype(jnp.bfloat16).astype(x.dtype)
            hs = jnp.square(jax.nn.relu(xf @ shared_w_up.T))
            shared_out = hs @ shared_w_down.T
            combined = jnp.zeros((flat_sel.shape[0], dim), routed_out.dtype).at[order].set(routed_out)
            out = combined.reshape(-1, TOP_K, dim).sum(axis=1) + shared_out
            return out.reshape(bs, slen, dim)
        key = jax.random.key(seed)
        k = jax.random.split(key, 6)
        s = 0.02
        return {'x': jax.random.normal(k[0], (BS, SLEN, DIM), jnp.float32), 'gate_w': jax.random.normal(k[1], (NUM_EXPERTS, DIM), jnp.float32) * s, 'expert_bias': jnp.zeros((NUM_EXPERTS,), jnp.float32), 'w_up': jax.random.normal(k[2], (NUM_EXPERTS, HID, DIM), jnp.float32) * s, 'w_down': jax.random.normal(k[3], (NUM_EXPERTS, DIM, HID), jnp.float32) * s, 'shared_w_up': jax.random.normal(k[4], (HID, DIM), jnp.float32) * s, 'shared_w_down': jax.random.normal(k[5], (DIM, HID), jnp.float32) * s}
    _L0_ffn_all = _L0_ffn_setup()
    _L0_ffn_in = {k: v for k, v in _L0_ffn_all.items() if k in ('gate_w', 'expert_bias', 'w_up', 'w_down', 'shared_w_up', 'shared_w_down')}
    del _L0_ffn_all
    return {'x': x, 'src': src, 'dst': dst, 'edge_type_5': edge_type_5, 'L0_gnn_edge_type_weights': _L0_gnn_in['edge_type_weights'], 'L0_gnn_wq': _L0_gnn_in['wq'], 'L0_gnn_bq': _L0_gnn_in['bq'], 'L0_gnn_wk': _L0_gnn_in['wk'], 'L0_gnn_bk': _L0_gnn_in['bk'], 'L0_gnn_wv': _L0_gnn_in['wv'], 'L0_gnn_bv': _L0_gnn_in['bv'], 'L0_gnn_wiq': _L0_gnn_in['wiq'], 'L0_gnn_biq': _L0_gnn_in['biq'], 'L0_gnn_wik': _L0_gnn_in['wik'], 'L0_gnn_bik': _L0_gnn_in['bik'], 'L0_gnn_wiv': _L0_gnn_in['wiv'], 'L0_gnn_biv': _L0_gnn_in['biv'], 'L0_gnn_wo': _L0_gnn_in['wo'], 'L0_gnn_bo': _L0_gnn_in['bo'], 'L0_mix_Wq': _L0_mix_in['Wq'], 'L0_mix_Wkv': _L0_mix_in['Wkv'], 'L0_mix_Wo': _L0_mix_in['Wo'], 'L0_mix_ln_gamma': _L0_mix_in['ln_gamma'], 'L0_mix_ln_beta': _L0_mix_in['ln_beta'], 'L0_ffn_gate_w': _L0_ffn_in['gate_w'], 'L0_ffn_expert_bias': _L0_ffn_in['expert_bias'], 'L0_ffn_w_up': _L0_ffn_in['w_up'], 'L0_ffn_w_down': _L0_ffn_in['w_down'], 'L0_ffn_shared_w_up': _L0_ffn_in['shared_w_up'], 'L0_ffn_shared_w_down': _L0_ffn_in['shared_w_down']}

def reference(x, src, dst, edge_type_5, L0_gnn_edge_type_weights, L0_gnn_wq, L0_gnn_bq, L0_gnn_wk, L0_gnn_bk, L0_gnn_wv, L0_gnn_bv, L0_gnn_wiq, L0_gnn_biq, L0_gnn_wik, L0_gnn_bik, L0_gnn_wiv, L0_gnn_biv, L0_gnn_wo, L0_gnn_bo, L0_mix_Wq, L0_mix_Wkv, L0_mix_Wo, L0_mix_ln_gamma, L0_mix_ln_beta, L0_ffn_gate_w, L0_ffn_expert_bias, L0_ffn_w_up, L0_ffn_w_down, L0_ffn_shared_w_up, L0_ffn_shared_w_down):
    import jax
    import jax.numpy as jnp

    def _L0_gnn_ref(x, edge_index, edge_type, edge_type_weights, wq, bq, wk, bk, wv, bv, wiq, biq, wik, bik, wiv, biv, wo, bo):
        import jax, jax.numpy as jnp
        import numpy as np
        N = 96
        E = 3072
        IN_F = 1024
        OUT_F = 1024
        H = 16
        D = OUT_F // H
        NUM_ETYPES = 4

        def _build_mask(edge_index, edge_type, edge_type_weights, dtype):
            src, dst = (edge_index[0], edge_index[1])
            w = jax.nn.softplus(edge_type_weights)
            mask = jnp.full((N, N), -jnp.inf, dtype=dtype)
            mask = mask.at[src, dst].set(w[edge_type - 1])
            diag = jnp.diagonal(mask)
            idx = jnp.arange(N)
            mask = mask.at[idx, idx].set(jnp.where(jnp.isneginf(diag), w[3], diag))
            return mask
        q = x @ wq.T + bq
        k = x @ wk.T + bk
        v = x @ wv.T + bv
        q2 = (q @ wiq.T + biq).reshape(N, H, D).transpose(1, 0, 2)
        k2 = (k @ wik.T + bik).reshape(N, H, D).transpose(1, 0, 2)
        v2 = (v @ wiv.T + biv).reshape(N, H, D).transpose(1, 0, 2)
        mask = _build_mask(edge_index, edge_type, edge_type_weights, x.dtype)
        scale = 1.0 / np.sqrt(D).astype(np.float32)
        scores = jnp.einsum('hnd,hmd->hnm', q2, k2) * scale + mask[None]
        attn = jax.nn.softmax(scores, axis=-1)
        out = jnp.einsum('hnm,hmd->hnd', attn, v2)
        out = out.transpose(1, 0, 2).reshape(N, OUT_F)
        return out @ wo.T + bo

    def _L0_mix_ref(h, Wq, Wkv, Wo, ln_gamma, ln_beta):
        import jax, jax.numpy as jnp
        import numpy as np
        N_HEAD = 16
        D_HEAD = 64
        D_MODEL = 1024
        N_ROLL = 3
        SCALE = 1.0 / D_HEAD ** 0.5
        EPS = 1e-05

        def mul_roll_repeat(x, n_roll):
            return jnp.concatenate([x * jnp.roll(x, i, axis=-1) for i in range(1, n_roll + 1)], axis=-1)

        def dpfp(x):
            x2 = jnp.concatenate([jax.nn.relu(x), jax.nn.relu(-x)], axis=-1)
            return mul_roll_repeat(x2, N_ROLL)

        def layer_norm(x, gamma, beta):
            mu = jnp.mean(x, axis=-1, keepdims=True)
            var = jnp.var(x, axis=-1, keepdims=True)
            return (x - mu) * jax.lax.rsqrt(var + 1e-05) * gamma + beta
        S, B, _ = h.shape
        q = (h @ Wq).reshape(S, B, N_HEAD, D_HEAD)
        kv = h @ Wkv
        k, v = jnp.split(kv, 2, axis=-1)
        k = k.reshape(S, B, N_HEAD, D_HEAD)
        v = v.reshape(S, B, N_HEAD, D_HEAD)
        pq = dpfp(q)
        pk = dpfp(k)
        kv_agg = jnp.einsum('jbnf,jbnd->bnfd', pk, v)
        z = pk.sum(axis=0)
        num = jnp.einsum('ibnf,bnfd->ibnd', pq, kv_agg) * SCALE
        den = jnp.einsum('ibnf,bnf->ibn', pq, z) * SCALE + EPS
        attn_vec = (num / den[..., None]).reshape(S, B, N_HEAD * D_HEAD)
        attn_out = attn_vec @ Wo
        return layer_norm(h + attn_out, ln_gamma, ln_beta)

    def _L0_ffn_ref(x, gate_w, expert_bias, w_up, w_down, shared_w_up, shared_w_down):
        import jax, jax.numpy as jnp
        import numpy as np
        BS, SLEN, DIM = (1, 64, 1024)
        NUM_EXPERTS, TOP_K = (8, 2)
        HID = 1408

        def _masked_grouped_mm(x, w, onehot):
            g = jnp.einsum('tk,gnk->tgn', x, w, preferred_element_type=jnp.float32)
            return jnp.einsum('tgn,tg->tn', g, onehot)

        def moe_forward(x, gate_w, expert_bias, w_up, w_down, shared_w_up, shared_w_down):
            bs, slen, dim = x.shape
            xf = x.reshape(-1, dim)
            scores = jax.nn.sigmoid((xf @ gate_w.T).astype(jnp.float32))
            biased = scores + expert_bias
            _, sel = jax.lax.top_k(biased, TOP_K)
            top_scores = jnp.take_along_axis(scores, sel, axis=-1)
            flat_sel = sel.reshape(-1)
            counts = jnp.bincount(flat_sel, length=NUM_EXPERTS)
            order = jnp.argsort(flat_sel, stable=True)
            scores_sorted = top_scores.reshape(-1)[order]
            token_ids = order // TOP_K
            routed_in = (xf[token_ids] * scores_sorted[:, None]).astype(x.dtype)
            seg = jnp.repeat(jnp.arange(NUM_EXPERTS), counts, total_repeat_length=flat_sel.shape[0])
            onehot = jax.nn.one_hot(seg, NUM_EXPERTS, dtype=jnp.float32)
            h = _masked_grouped_mm(routed_in.astype(jnp.bfloat16), w_up.astype(jnp.bfloat16), onehot)
            h = jnp.square(jax.nn.relu(h.astype(jnp.bfloat16)))
            routed_out = _masked_grouped_mm(h.astype(jnp.bfloat16), w_down.astype(jnp.bfloat16), onehot)
            routed_out = routed_out.astype(jnp.bfloat16).astype(x.dtype)
            hs = jnp.square(jax.nn.relu(xf @ shared_w_up.T))
            shared_out = hs @ shared_w_down.T
            combined = jnp.zeros((flat_sel.shape[0], dim), routed_out.dtype).at[order].set(routed_out)
            out = combined.reshape(-1, TOP_K, dim).sum(axis=1) + shared_out
            return out.reshape(bs, slen, dim)
        return moe_forward(x, gate_w, expert_bias, w_up, w_down, shared_w_up, shared_w_down)
    edge_index = jnp.stack([src, dst])
    xn = _layernorm(x, axis=-1)
    x = x + _L0_gnn_ref(xn, edge_index, edge_type_5, L0_gnn_edge_type_weights, L0_gnn_wq, L0_gnn_bq, L0_gnn_wk, L0_gnn_bk, L0_gnn_wv, L0_gnn_bv, L0_gnn_wiq, L0_gnn_biq, L0_gnn_wik, L0_gnn_bik, L0_gnn_wiv, L0_gnn_biv, L0_gnn_wo, L0_gnn_bo) + _L0_mix_ref(xn[None], L0_mix_Wq, L0_mix_Wkv, L0_mix_Wo, L0_mix_ln_gamma, L0_mix_ln_beta)[0]
    x = x + _L0_ffn_ref(_layernorm(x, axis=-1)[None], L0_ffn_gate_w, L0_ffn_expert_bias, L0_ffn_w_up, L0_ffn_w_down, L0_ffn_shared_w_up, L0_ffn_shared_w_down)[0]
    return x

_drawn_inputs = setup_inputs


def setup_inputs(seed=0):
    import zlib

    import numpy as np

    out = dict(_drawn_inputs(seed))
    spreads = {'L0_mix_ln_gamma': (1.0, 0.2),
     'L0_mix_ln_beta': (0.0, 0.1),
     'L0_ffn_expert_bias': (0.0, 0.1)}
    factors = {'L0_gnn_edge_type_weights': 64.0,
     'L0_gnn_wq': 8.0,
     'L0_gnn_bq': 8.0,
     'L0_gnn_wk': 6.255,
     'L0_gnn_bk': 64.0,
     'L0_gnn_bv': 8.0,
     'L0_gnn_wiq': 8.0,
     'L0_gnn_biq': 35.64,
     'L0_gnn_wik': 8.0,
     'L0_gnn_bik': 64.0,
     'L0_gnn_biv': 6.837,
     'L0_gnn_bo': 4.47,
     'L0_mix_Wq': 64.0}
    for name, (base, spread) in spreads.items():
        noise = np.random.default_rng([zlib.crc32(name.encode()), seed]).standard_normal(out[name].shape)
        drawn = base * np.exp(spread * noise) if base else spread * noise
        out[name] = jnp.asarray(drawn.astype(out[name].dtype))
    for name, factor in factors.items():
        out[name] = (out[name] * factor).astype(out[name].dtype)
    return out
```

```python
from contextlib import ExitStack

import concourse.bass as bass
from concourse import mybir

F32 = mybir.dt.float32
BF16 = mybir.dt.bfloat16
I32 = mybir.dt.int32
ALU = mybir.AluOpType
ACT = mybir.ActivationFunctionType
AX_X = mybir.AxisListType.X

P = 128
N = 96
D = 1024
KT = D // P
HALF = D // 2
HT = HALF // P
H = 16
DH = D // H
PAIR = H // 2
EDGES = 3072
EC = EDGES // P
ETYPES = 4
HID = 1408
TT = HID // P
EXPERTS = 8
EPS = 1e-5
SCALE = 1.0 / DH ** 0.5
ROLL = 3
FEAT = 2 * DH
ABSENT = 1.0e30

GROUP = 4
SLOT = KT * HALF
SLOTS = 5
UNIT = D
TILES = [(0, 4), (4, 8), (8, 11)]
PARTS = len(TILES)

MATS = ["wq", "wk", "wv", "wiq", "wik", "wiv", "mq", "mk", "mv"]
STEPS = [(m, h) for m in MATS for h in range(2)] + [("wo", 0), ("mo", 0), ("mo", 1), ("wo", 1)]
AT = {s: c for c, s in enumerate(STEPS)}
BANKS = {m: 2 * (i % 2) for i, m in enumerate(MATS)} | {"wo": 0, "mo": 2}
BIASES = ["wq", "wk", "wv", "wiq", "wik"]


def gps_layer(nc, x, mats, bias_cols, bias_v, bias_o, ln_gamma, ln_beta, src_rows, dst_rows,
              src_cols, dst_cols, type_cols, edge_w, gate_w, expert_bias, shared_up, shared_down,
              expert_up, expert_down, out):
    ctx = ExitStack()
    with ctx:
        def sb(name, shape, dt):
            return ctx.enter_context(nc.sbuf_tensor(name, shape, dt))

        def sem(name):
            return ctx.enter_context(nc.semaphore(name))

        bank = [ctx.enter_context(nc.psum_tensor(f"bank{i}", [P, 512], F32)) for i in range(8)]

        ring = sb("ring", [P, 2 * TT * UNIT], F32)
        stage = [sb(f"stage{b}", [P, TT * UNIT], F32) for b in range(2)]
        slots = [ring[:, s * SLOT:(s + 1) * SLOT].rearrange("p (k n) -> p k n", k=KT)
                 for s in range(SLOTS)]
        tail = SLOTS * SLOT
        gamma = ring[:, tail:tail + D]
        beta = ring[:, tail + D:tail + 2 * D]
        sh_up = ring[:, 2 * SLOT:2 * SLOT + TT * UNIT]
        sh_up_t = sh_up.rearrange("p (t k j) -> p t k j", t=TT, k=KT)
        end = 2 * SLOT + TT * UNIT
        sh_dn = [ring[:, end:end + 3 * UNIT], ring[:, 0:4 * UNIT], ring[:, 4 * UNIT:8 * UNIT]]
        SH_DN_TILES = [(0, 3), (3, 7), (7, 11)]

        arena = stage[1]

        def take(at, n):
            return arena[:, at:at + n]

        scores = take(0, H * N)
        attn_t = take(1536, H * N)
        q1 = take(3072, KT * N)
        k1 = take(3840, KT * N)
        v1 = take(4608, KT * N)
        q2 = take(5376, KT * N)
        k2 = take(6144, KT * N)
        v2 = take(6912, D)
        prod = take(7936, H * (FEAT + ROLL))
        relu_q = take(10032, D)
        rolled = take(3072, H * FEAT)
        neg_q = take(5376, D)
        mvec = take(7936, D)
        mvec_t = take(10032, KT * N)
        out_t = take(5376, KT * N)
        bias_o_b = take(0, D)
        bias_v_b = take(10032, D)
        oh_src = take(1536, EC * N // 2).bitcast(BF16).rearrange("p (c s) -> p c s", c=EC)
        oh_dst = take(7936, EC * N // 2).bitcast(BF16).rearrange("p (c s) -> p c s", c=EC)
        same = take(0, P)

        def tiles(ap):
            return ap.rearrange("p (k n) -> p k n", n=N)

        xs = sb("xs", [P, TT * N], F32)
        xn = sb("xn", [P, D], F32)
        xnt = sb("xnt", [P, KT * N], F32)
        acc = sb("acc", [P, D], F32)
        hbuf = sb("hbuf", [P, TT * N], F32)
        xe = sb("xe", [P, KT * N], BF16)
        rounded = sb("rounded", [P, D], BF16)
        w_all = sb("w_all", [P, EXPERTS, N], F32)
        sh_h = xs[:, :]
        sh_relu = hbuf[:, :]
        e_h = hbuf[:, 0:TT * N // 2].bitcast(BF16)
        e_relu = xn[:, 0:TT * N // 2].bitcast(BF16)

        ident = sb("ident", [P, P], F32)
        lower = sb("lower", [P, EXPERTS, EXPERTS], F32)
        iota_i = sb("iota_i", [P, N], I32)
        iota = sb("iota", [P, N], F32)
        codebase_i = sb("codebase_i", [P, EC], I32)
        bias_c = sb("bias_c", [P, len(BIASES) * KT], F32)
        gate = sb("gate", [P, KT * EXPERTS], F32)
        ebias = sb("ebias", [P, EXPERTS], F32)
        ew = sb("ew", [P, ETYPES], F32)
        later = acc[:, 0:P]
        src_r = acc[0:EC, P:2 * P].bitcast(I32)
        dst_r = acc[0:EC, 2 * P:3 * P].bitcast(I32)
        key_r = acc[0:EC, 3 * P:4 * P]
        edge_c = acc[:, 4 * P:4 * P + 3 * EC].bitcast(I32).rearrange("p (r c) -> p r c", r=3)
        edge_f = acc[:, 6 * P:6 * P + 8 * EC].rearrange("p (r c) -> p r c", r=8)
        code = hbuf[:, 0:2 * N].rearrange("p (r n) -> p r n", r=2)
        mtmp = hbuf[:, 2 * N:4 * N].rearrange("p (r n) -> p r n", r=2)
        code_i = hbuf[:, 4 * N:5 * N].bitcast(I32)
        mask = sb("mask", [P, N], F32)
        small = sb("small", [P, 64], F32)
        stat = sb("stat", [P, 2, 6], F32)
        head = sb("head", [P, 6, H], F32)
        route = sb("route", [P, 8, EXPERTS], F32)
        beat = sb("beat", [P, 2, EXPERTS * EXPERTS], F32)

        x_landed = sem("x_landed")
        rows_landed = sem("rows_landed")
        cols_landed = sem("cols_landed")
        bias_landed = sem("bias_landed")
        bias_v_landed = sem("bias_v_landed")
        ln_landed = sem("ln_landed")
        bias_o_landed = sem("bias_o_landed")
        gate_landed = sem("gate_landed")
        slot_landed = [sem(f"slot_landed{s}") for s in range(SLOTS)]
        shared_landed = [sem(f"shared_landed{j}") for j in range(2 * PARTS)]
        stage_landed = [[sem(f"stage_landed{b}_{j}") for j in range(2 * PARTS)] for b in range(2)]
        out_landed = sem("out_landed")
        pool_step = sem("pool_step")
        spread = sem("spread")
        dve_step = sem("dve_step")
        act_step = sem("act_step")
        key_ready = sem("key_ready")
        key_psum = sem("key_psum")
        key_used = sem("key_used")
        onehot_ready = sem("onehot_ready")
        code_psum = sem("code_psum")
        code_used = sem("code_used")
        soft_in = sem("soft_in")
        soft_log = sem("soft_log")
        var1_ready = sem("var1_ready")
        std1_ready = sem("std1_ready")
        xn_ready = sem("xn_ready")
        xnt_psum = sem("xnt_psum")
        xnt_ready = sem("xnt_ready")
        half_done = sem("half_done")
        half_out = sem("half_out")
        scores_psum = sem("scores_psum")
        shifted = sem("shifted")
        exps_ready = sem("exps_ready")
        attn_ready = sem("attn_ready")
        attn_t_psum = sem("attn_t_psum")
        attn_t_ready = sem("attn_t_ready")
        pv_psum = sem("pv_psum")
        out_t_ready = sem("out_t_ready")
        relu_q_ready = sem("relu_q_ready")
        prod_ready = sem("prod_ready")
        mvec_ready = sem("mvec_ready")
        mvec_t_psum = sem("mvec_t_psum")
        mvec_t_ready = sem("mvec_t_ready")
        varm_ready = sem("varm_ready")
        stdm_ready = sem("stdm_ready")
        pre_ready = sem("pre_ready")
        var2_ready = sem("var2_ready")
        std2_ready = sem("std2_ready")
        xn2_ready = sem("xn2_ready")
        xn2t_psum = sem("xn2t_psum")
        xn2t_ready = sem("xn2t_ready")
        logits_psum = sem("logits_psum")
        gate_exp = sem("gate_exp")
        route_ready = sem("route_ready")
        w_all_psum = sem("w_all_psum")
        w_all_ready = sem("w_all_ready")
        xe_ready = sem("xe_ready")
        up_done = sem("up_done")
        relu_done = sem("relu_done")
        h_ready = sem("h_ready")
        down_done = sem("down_done")
        free23 = sem("free23")
        free01 = sem("free01")
        added = sem("added")

        block = ctx.enter_context(nc.Block())

        def half_landed(eng, c):
            eng.wait_ge(slot_landed[c % SLOTS], 16 * (c // SLOTS + 1))

        @block.sync
        def _(sp):
            sp.dma_start(xs[0:N, 0:D], x).then_inc(x_landed, 16)
            for c, (m, h) in enumerate(STEPS):
                if c >= SLOTS:
                    sp.wait_ge(half_done, c - SLOTS + 1)
                dst = ring[:, (c % SLOTS) * SLOT:(c % SLOTS + 1) * SLOT]
                sp.dma_start(dst, mats[m][h]).then_inc(slot_landed[c % SLOTS], 16)
            last = {c % SLOTS: c for c in range(len(STEPS))}
            for j, (t0, t1) in enumerate(TILES):
                sp.wait_ge(half_done, last[2 + j] + 1)
                sp.dma_start(sh_up[:, t0 * UNIT:t1 * UNIT], shared_up[:, t0 * UNIT:t1 * UNIT])\
                  .then_inc(shared_landed[j], 16)
            for j, (t0, t1) in enumerate(SH_DN_TILES):
                if j == 0:
                    sp.wait_ge(pre_ready, 1)
                else:
                    sp.wait_ge(half_done, last[j - 1] + 1)
                sp.dma_start(sh_dn[j], shared_down[:, t0 * UNIT:t1 * UNIT])\
                  .then_inc(shared_landed[PARTS + j], 16)
            for h in range(2):
                sp.wait_ge(added, 2 * EXPERTS + 1 + h)
                if h == 1:
                    sp.wait_ge(added, 2 * EXPERTS + 2)
                sp.dma_start(out[:, h * HALF:(h + 1) * HALF], acc[0:N, h * HALF:(h + 1) * HALF])\
                  .then_inc(out_landed, 16)
            sp.wait_ge(out_landed, 32)

        @block.gpsimd
        def _(pool):
            nc.gpsimd.memset(ident[:], 0.0).then_inc(pool_step, 1)
            pool.wait_ge(pool_step, 1)
            nc.gpsimd.affine_select(out=ident[:], in_=ident[:], compare_op=ALU.not_equal, fill=1.0,
                                    base=0, pattern=[[-1, P]], channel_multiplier=1)\
              .then_inc(pool_step, 1)
            nc.gpsimd.memset(later, 1.0).then_inc(pool_step, 1)
            pool.wait_ge(pool_step, 3)
            nc.gpsimd.affine_select(out=later, in_=later, compare_op=ALU.is_gt, fill=0.0,
                                    base=0, pattern=[[1, P]], channel_multiplier=-1)\
              .then_inc(pool_step, 1)
            nc.gpsimd.iota(iota_i[:], pattern=[[1, N]], base=0, channel_multiplier=0)\
              .then_inc(pool_step, 1)
            nc.gpsimd.iota(codebase_i[:], pattern=[[ETYPES, EC]], base=0, channel_multiplier=0)\
              .then_inc(pool_step, 1)
            nc.gpsimd.memset(lower[:], 1.0).then_inc(pool_step, 1)
            pool.wait_ge(pool_step, 7)
            nc.gpsimd.affine_select(out=lower[:], in_=lower[:], compare_op=ALU.is_gt, fill=0.0,
                                    base=0, pattern=[[1, EXPERTS], [-1, EXPERTS]],
                                    channel_multiplier=0).then_inc(pool_step, 1)
            pool.wait_ge(bias_v_landed, 16)
            nc.gpsimd.partition_broadcast(bias_v_b, bias_v_b[0:1, :]).then_inc(spread, 1)
            pool.wait_ge(ln_landed, 32)
            nc.gpsimd.partition_broadcast(gamma, gamma[0:1, :]).then_inc(spread, 1)
            nc.gpsimd.partition_broadcast(beta, beta[0:1, :]).then_inc(spread, 1)

            halves = [stage[b][:, :].rearrange("p (m n) -> p m n", m=2) for b in range(2)]

            def buffer(b, m, t0, t1):
                return halves[b][:, m, :].bitcast(BF16)[:, t0 * UNIT:t1 * UNIT]

            for m, weights in enumerate((expert_up, expert_down)):
                for j, (t0, t1) in enumerate(TILES):
                    pool.wait_ge(half_done, 4 + 2 * (PARTS * m + j))
                    pool.dma_start(buffer(0, m, t0, t1), weights[0, :, t0 * UNIT:t1 * UNIT])\
                        .then_inc(stage_landed[0][PARTS * m + j], 16)
            pool.wait_ge(pv_psum, 2)
            pool.wait_ge(bias_o_landed, 16)
            nc.gpsimd.partition_broadcast(bias_o_b, bias_o_b[0:1, :]).then_inc(spread, 1)
            pool.wait_ge(pre_ready, 1)
            pool.wait_ge(half_done, len(STEPS))
            for m, weights in enumerate((expert_up, expert_down)):
                for j, (t0, t1) in enumerate(TILES):
                    pool.dma_start(buffer(1, m, t0, t1), weights[1, :, t0 * UNIT:t1 * UNIT])\
                        .then_inc(stage_landed[1][PARTS * m + j], 16)
            with pool.Fori(1, EXPERTS // 2) as i:
                for b in range(2):
                    for m, (weights, done) in enumerate(((expert_up, up_done),
                                                         (expert_down, down_done))):
                        for j, (t0, t1) in enumerate(TILES):
                            pool.wait_ge(pre_ready, 1)
                            pool.wait_ge(done, i * (2 * PARTS) + (PARTS * (b - 1) + j + 1))
                            pool.dma_start(buffer(b, m, t0, t1),
                                           weights[bass.ds(i * 2 + b, 1), :, t0 * UNIT:t1 * UNIT]
                                           .rearrange("a p n -> (a p) n"))\
                                .then_inc(stage_landed[b][PARTS * m + j], 16)

        @block.scalar
        def _(act):
            act.dma_start(src_r, src_rows).then_inc(rows_landed, 16)
            act.dma_start(dst_r, dst_rows).then_inc(rows_landed, 16)
            act.dma_start(edge_c[:, 0, :], src_cols).then_inc(cols_landed, 16)
            act.dma_start(edge_c[:, 1, :], dst_cols).then_inc(cols_landed, 16)
            act.dma_start(edge_c[:, 2, :], type_cols).then_inc(cols_landed, 16)
            act.dma_start(ew[:, :], edge_w.broadcast_to([P, ETYPES])).then_inc(cols_landed, 16)
            act.dma_start(bias_c[:], bias_cols).then_inc(bias_landed, 16)
            act.dma_start(bias_v_b[0:1, :], bias_v).then_inc(bias_v_landed, 16)
            act.dma_start(gamma[0:1, :], ln_gamma).then_inc(ln_landed, 16)
            act.dma_start(beta[0:1, :], ln_beta).then_inc(ln_landed, 16)
            act.dma_start(gate[:], gate_w).then_inc(gate_landed, 16)
            act.dma_start(ebias[:], expert_bias.broadcast_to([P, EXPERTS])).then_inc(gate_landed, 16)

            act.wait_ge(var1_ready, 1)
            nc.scalar.activation(small[0:N, 3:4], small[0:N, 2:3], ACT.Sqrt).then_inc(std1_ready, 1)
            for b in range(2):
                act.wait_ge(xnt_psum, b + 1)
                nc.scalar.activation(xnt[:, b * GROUP * N:(b + 1) * GROUP * N],
                                     bank[4 + b][:, 0:GROUP * N], ACT.Copy).then_inc(xnt_ready, 1)
            act.wait_ge(soft_in, 1)
            nc.scalar.activation(small[:, 20:24], small[:, 16:20], ACT.Exp, scale=-1.0)\
              .then_inc(act_step, 1)
            act.wait_ge(act_step, 1)
            nc.scalar.activation(small[:, 24:28], small[:, 20:24], ACT.Ln, bias=small[:, 28:29])\
              .then_inc(soft_log, 1)
            act.wait_ge(shifted, 1)
            nc.scalar.activation(scores[0:N, :], scores[0:N, :], ACT.Exp).then_inc(exps_ready, 1)
            for h in range(2):
                act.wait_ge(half_done, AT["mq", h] + 1)
                if h == 0:
                    act.wait_ge(half_out, AT["wiv", 1] + 1)
                nc.scalar.activation(relu_q[0:N, h * HALF:(h + 1) * HALF],
                                     bank[BANKS["mq"] + h][0:N, :], ACT.Relu).then_inc(relu_q_ready, 1)
            for b in range(4):
                act.wait_ge(attn_t_psum, b + 1)
                nc.scalar.activation(attn_t[0:N, b * GROUP * N:(b + 1) * GROUP * N],
                                     bank[4 + b][0:N, 0:GROUP * N], ACT.Copy)\
                  .then_inc(attn_t_ready, 1)
            act.wait_ge(prod_ready, 1)
            for b in range(2):
                act.wait_ge(pv_psum, b + 1)
                nc.scalar.activation(out_t[:, b * GROUP * N:(b + 1) * GROUP * N],
                                     bank[4 + b][:, 0:GROUP * N], ACT.Copy)\
                  .then_inc(out_t_ready, 1)
            act.dma_start(bias_o_b[0:1, :], bias_o).then_inc(bias_o_landed, 16)
            for b in range(2):
                act.wait_ge(mvec_t_psum, b + 1)
                nc.scalar.activation(mvec_t[:, b * GROUP * N:(b + 1) * GROUP * N],
                                     bank[6 + b][:, 0:GROUP * N], ACT.Copy)\
                  .then_inc(mvec_t_ready, 1)
            act.wait_ge(varm_ready, 1)
            nc.scalar.activation(small[0:N, 35:36], small[0:N, 34:35], ACT.Sqrt).then_inc(stdm_ready, 1)
            act.wait_ge(var2_ready, 1)
            nc.scalar.activation(small[0:N, 43:44], small[0:N, 42:43], ACT.Sqrt).then_inc(std2_ready, 1)
            for b in range(2):
                act.wait_ge(xn2t_psum, b + 1)
                nc.scalar.activation(xnt[:, b * GROUP * N:(b + 1) * GROUP * N],
                                     bank[2 + b][:, 0:GROUP * N], ACT.Copy).then_inc(xn2t_ready, 1)
            act.wait_ge(logits_psum, 1)
            nc.scalar.activation(route[0:N, 0, :], bank[7][0:N, 0:EXPERTS], ACT.Exp, scale=-1.0)\
              .then_inc(gate_exp, 1)
            for j, (t0, t1) in enumerate(TILES):
                act.wait_ge(up_done, j + 1)
                nc.scalar.activation(sh_relu[:, t0 * N:t1 * N], bank[4 + j][:, 0:(t1 - t0) * N],
                                     ACT.Relu).then_inc(relu_done, 1)

            def expert(i, b):
                for j, (t0, t1) in enumerate(TILES):
                    act.wait_ge(up_done, i * (2 * PARTS) + (PARTS * (b + 1) + j + 1))
                    if j == 0:
                        act.wait_ge(h_ready, i * (2 * PARTS) + PARTS * (b + 1))
                    nc.scalar.activation(e_relu[:, t0 * N:t1 * N], bank[4 + j][:, 0:(t1 - t0) * N],
                                         ACT.Relu).then_inc(relu_done, 1)
                act.wait_ge(down_done, i * (2 * PARTS) + PARTS * (b + 2))
                act.wait_ge(added, i * 4 + 2 * (b + 1))
                for h in range(2):
                    nc.scalar.activation(rounded[0:N, h * HALF:(h + 1) * HALF],
                                         bank[2 * (1 - b) + h][0:N, :], ACT.Copy)\
                      .then_inc(free01 if b else free23, 1)

            with act.Fori(0, EXPERTS // 2) as i:
                for b in range(2):
                    expert(i, b)

        @block.vector
        def _(dve):
            chain = [0]

            def link(ins):
                chain[0] += 1
                ins.then_inc(dve_step, 1)
                dve.wait_ge(dve_step, chain[0])

            tt, ts, stt = nc.vector.tensor_tensor, nc.vector.tensor_scalar, nc.vector.scalar_tensor_tensor

            def layernorm_stats(src, at, ready):
                for h in range(2):
                    ins = nc.vector.bn_stats(stat[0:N, h, :], src[0:N, h * HALF:(h + 1) * HALF])
                    if h == 1:
                        link(ins)
                link(nc.vector.bn_aggr(small[0:N, at:at + 2], stat[0:N, :, :]))
                ts(small[0:N, at + 2:at + 3], small[0:N, at + 1:at + 2], EPS, None, ALU.add)\
                    .then_inc(ready, 1)

            dve.wait_ge(rows_landed, 32)
            link(stt(key_r, src_r, float(N), dst_r, ALU.mult, ALU.add))
            nc.vector.memset(small[:, 28:29], 1.0).then_inc(key_ready, 1)

            dve.wait_ge(x_landed, 16)
            layernorm_stats(xs, 0, var1_ready)
            dve.wait_ge(cols_landed, 64)
            SRC, DST, TYP, KEY, LAST, VAL, TMP, BASE = range(8)
            nc.vector.tensor_copy(edge_f[:, SRC:TYP + 1, :], edge_c[:, :, :]).then_inc(dve_step, 1)
            dve.wait_ge(dve_step, chain[0] + 1)
            chain[0] += 1
            dve.wait_ge(std1_ready, 1)
            link(nc.vector.reciprocal(small[0:N, 4:5], small[0:N, 3:4]))
            for h in range(2):
                ts(xn[0:N, h * HALF:(h + 1) * HALF], xs[0:N, h * HALF:(h + 1) * HALF], small[0:N, 0:1],
                   small[0:N, 4:5], ALU.subtract, ALU.mult).then_inc(xn_ready, 1)
            link(stt(edge_f[:, KEY, :], edge_f[:, SRC, :], float(N), edge_f[:, DST, :],
                     ALU.mult, ALU.add))
            link(ts(small[:, 12:16], ew[:], -1.0, None, ALU.mult))
            tt(small[:, 16:20], ew[:], small[:, 12:16], ALU.max).then_inc(soft_in, 1)
            dve.wait_ge(pool_step, 8)
            for r in range(EC // GROUP):
                dve.wait_ge(key_psum, r + 1)
                if r:
                    dve.wait_ge(key_used, r)
                for g in range(GROUP):
                    c = r * GROUP + g
                    ins = stt(same, bank[6 + r % 2][:, g * P:(g + 1) * P],
                              edge_f[:, KEY, c:c + 1], later, ALU.is_equal, ALU.mult,
                              accum_out=edge_f[:, LAST, c:c + 1])
                    if g == GROUP - 1:
                        ins.then_inc(key_used, 1)
                    else:
                        link(ins)
            dve.wait_ge(key_used, EC // GROUP)
            link(ts(edge_f[:, LAST, :], edge_f[:, LAST, :], 0.0, None, ALU.is_equal))
            link(ts(edge_f[:, TMP, :], edge_f[:, TYP, :], 0.0, float(ETYPES), ALU.is_equal, ALU.mult))
            link(tt(edge_f[:, VAL, :], edge_f[:, TMP, :], edge_f[:, TYP, :], ALU.add))
            nc.vector.tensor_copy(iota[:], iota_i[:])
            link(nc.vector.tensor_copy(edge_f[:, BASE, :], codebase_i[:]))
            link(tt(edge_f[:, VAL, :], edge_f[:, VAL, :], edge_f[:, BASE, :], ALU.add))
            link(tt(edge_f[:, VAL, :], edge_f[:, VAL, :], edge_f[:, LAST, :], ALU.mult))

            def by_node(row):
                return edge_f[:, row, :].unsqueeze(2).broadcast_to([P, EC, N])

            iota_b = iota[:].unsqueeze(1).broadcast_to([P, EC, N])
            link(tt(oh_dst, iota_b, by_node(DST), ALU.is_equal))
            link(tt(oh_src, iota_b, by_node(SRC), ALU.is_equal))
            tt(oh_src, oh_src, by_node(VAL), ALU.mult).then_inc(onehot_ready, 1)

            def take_t(m, h, dst):
                c = AT[m, h]
                dve.wait_ge(half_done, c + 1)
                at = BIASES.index(m) * KT + h * HT
                b = bias_c[:, at:at + HT].unsqueeze(2).broadcast_to([P, HT, N])
                tt(tiles(dst)[:, h * HT:(h + 1) * HT, :],
                   tiles(bank[BANKS[m] + h][:, 0:HT * N]), b, ALU.add).then_inc(half_out, 1)

            def codes(r):
                c0, c1 = 5 * r, min(5 * r + 5, EC)
                dve.wait_ge(code_psum, r + 1)
                v = bank[4 + r % 2][0:N, 0:(c1 - c0) * N].rearrange("s (c d) -> s d c", d=N)
                nc.vector.tensor_reduce(code[0:N, 1 if r else 0, :], v, AX_X, ALU.max)\
                    .then_inc(code_used, 1)
                if r:
                    dve.wait_ge(code_used, r + 1)
                    link(tt(code[0:N, 0, :], code[0:N, 0, :], code[0:N, 1, :], ALU.max))

            dve.wait_ge(bias_landed, 16)
            for r in range(5):
                codes(r)
            link(ts(mtmp[0:N, 0, :], code[0:N, 0, :], 0.0, None, ALU.is_gt))
            link(ts(code_i[0:N, :], code[0:N, 0, :], float(ETYPES - 1), None, ALU.add))
            link(ts(code_i[0:N, :], code_i[0:N, :], ETYPES - 1, None, ALU.bitwise_and))
            link(nc.vector.tensor_copy(code[0:N, 1, :], code_i[0:N, :]))
            dve.wait_ge(soft_log, 1)
            link(ts(small[:, 12:16], ew[:], 0.0, None, ALU.max))
            link(tt(small[:, 12:16], small[:, 12:16], small[:, 24:28], ALU.add))
            for k in range(ETYPES):
                w = small[0:N, 12 + k:13 + k]
                if k == 0:
                    link(ts(mask[0:N, :], code[0:N, 1, :], float(k), w, ALU.is_equal, ALU.mult))
                else:
                    link(ts(mtmp[0:N, 1, :], code[0:N, 1, :], float(k), w, ALU.is_equal, ALU.mult))
                    link(tt(mask[0:N, :], mask[0:N, :], mtmp[0:N, 1, :], ALU.add))
            link(tt(mask[0:N, :], mask[0:N, :], mtmp[0:N, 0, :], ALU.mult))
            link(ts(mtmp[0:N, 1, :], ident[0:N, 0:N], 1.0, ABSENT, ALU.subtract, ALU.mult))
            link(stt(mtmp[0:N, 1, :], ident[0:N, 0:N], small[0:N, 15:16], mtmp[0:N, 1, :],
                     ALU.mult, ALU.add))
            link(ts(mtmp[0:N, 0, :], mtmp[0:N, 0, :], -1.0, 1.0, ALU.mult, ALU.add))
            link(tt(mtmp[0:N, 1, :], mtmp[0:N, 1, :], mtmp[0:N, 0, :], ALU.mult))
            link(tt(mask[0:N, :], mask[0:N, :], mtmp[0:N, 1, :], ALU.add))

            for m, dst in (("wq", q1), ("wk", k1), ("wv", v1), ("wiq", q2), ("wik", k2)):
                for h in range(2):
                    take_t(m, h, dst)
            dve.wait_ge(spread, 1)
            for h in range(2):
                dve.wait_ge(half_done, AT["wiv", h] + 1)
                cols = slice(h * HALF, (h + 1) * HALF)
                tt(v2[0:N, cols], bank[BANKS["wiv"] + h][0:N, :], bias_v_b[0:N, cols], ALU.add)\
                    .then_inc(half_out, 1)

            sc = tiles(scores[0:N, :])
            for b in (0, 2, 1, 3):
                dve.wait_ge(scores_psum, b % 2 + 1)
                ins = stt(sc[:, b * GROUP:(b + 1) * GROUP, :], tiles(bank[4 + b][0:N, 0:GROUP * N]),
                          SCALE, mask[0:N, :].unsqueeze(1).broadcast_to([N, GROUP, N]),
                          ALU.mult, ALU.add)
                link(ins)
            MX, SUM, INV = range(3)

            def by_head(row, n):
                return head[0:N, row, :].unsqueeze(2).broadcast_to([N, H, n])

            link(nc.vector.tensor_reduce(head[0:N, MX, :], sc, AX_X, ALU.max))
            tt(sc, sc, by_head(MX, N), ALU.subtract).then_inc(shifted, 1)

            for h in range(2):
                dve.wait_ge(relu_q_ready, h + 1)
                cols = slice(h * HALF, (h + 1) * HALF)
                ts(neg_q[0:N, cols], bank[BANKS["mq"] + h][0:N, :], 0.0, None, ALU.min)\
                    .then_inc(half_out, 1)
            dve.wait_ge(exps_ready, 1)
            link(nc.vector.tensor_reduce(head[0:N, SUM, :], sc, AX_X, ALU.add))
            link(nc.vector.reciprocal(head[0:N, INV, :], head[0:N, SUM, :]))
            tt(sc, sc, by_head(INV, N), ALU.mult).then_inc(attn_ready, 1)

            pr = prod[0:N, :].rearrange("n (h f) -> n h f", h=H)
            dve.wait_ge(half_out, AT["mq", 1] + 1)
            for h in range(2):
                dve.wait_ge(half_done, AT["mk", h] + 1)
                heads = slice(h * H // 2, (h + 1) * H // 2)
                cols = slice(h * HALF, (h + 1) * HALF)
                k_ps = bank[BANKS["mk"] + h][0:N, :].rearrange("n (h f) -> n h f", f=DH)
                stt(pr[:, heads, ROLL:ROLL + DH], k_ps, 0.0,
                    relu_q[0:N, cols].rearrange("n (h f) -> n h f", f=DH), ALU.max, ALU.mult)
                ins = stt(pr[:, heads, ROLL + DH:ROLL + FEAT], k_ps, 0.0,
                          neg_q[0:N, cols].rearrange("n (h f) -> n h f", f=DH), ALU.min, ALU.mult)
                ins.then_inc(half_out, 1)
            dve.wait_ge(half_out, AT["mk", 1] + 1)
            nc.vector.tensor_copy(pr[:, :, 0:ROLL], pr[:, :, FEAT:FEAT + ROLL]).then_inc(prod_ready, 1)
            dve.wait_ge(prod_ready, 1)
            ro = rolled[0:N, :].rearrange("n (h f) -> n h f", h=H)
            link(tt(ro, pr[:, :, 2:2 + FEAT], pr[:, :, 1:1 + FEAT], ALU.add))
            link(tt(ro, ro, pr[:, :, 0:FEAT], ALU.add))
            link(tt(ro, ro, pr[:, :, ROLL:ROLL + FEAT], ALU.mult))
            S, DEN, RDEN = 3, 4, 5
            link(nc.vector.tensor_reduce(head[0:N, S, :], ro, AX_X, ALU.add))
            link(ts(head[0:N, DEN, :], head[0:N, S, :], SCALE, EPS, ALU.mult, ALU.add))
            link(nc.vector.reciprocal(head[0:N, RDEN, :], head[0:N, DEN, :]))
            link(stt(head[0:N, S, :], head[0:N, S, :], SCALE, head[0:N, RDEN, :],
                     ALU.mult, ALU.mult))
            for h in range(2):
                dve.wait_ge(half_done, AT["mv", h] + 1)
                heads = slice(h * H // 2, (h + 1) * H // 2)
                cols = slice(h * HALF, (h + 1) * HALF)
                tt(mvec[0:N, cols].rearrange("n (h f) -> n h f", f=DH),
                   bank[BANKS["mv"] + h][0:N, :].rearrange("n (h f) -> n h f", f=DH),
                   by_head(S, DH)[:, heads, :], ALU.mult).then_inc(half_out, 1)

            for h in range(2):
                dve.wait_ge(half_done, AT["mo", h] + 1)
                cols = slice(h * HALF, (h + 1) * HALF)
                ins = tt(acc[0:N, cols], bank[BANKS["mo"] + h][0:N, :], xn[0:N, cols], ALU.add)
                link(ins)
            layernorm_stats(acc, 32, varm_ready)
            dve.wait_ge(stdm_ready, 1)
            link(nc.vector.reciprocal(small[0:N, 36:37], small[0:N, 35:36]))
            link(ts(acc[0:N, :], acc[0:N, :], small[0:N, 32:33], small[0:N, 36:37],
                    ALU.subtract, ALU.mult))
            dve.wait_ge(spread, 3)
            link(tt(acc[0:N, :], acc[0:N, :], gamma[0:N, :], ALU.mult))
            link(tt(acc[0:N, :], acc[0:N, :], beta[0:N, :], ALU.add))
            link(tt(acc[0:N, :], acc[0:N, :], xs[0:N, 0:D], ALU.add))
            dve.wait_ge(spread, 4)
            tt(acc[0:N, :], acc[0:N, :], bias_o_b[0:N, :], ALU.add).then_inc(pre_ready, 1)
            dve.wait_ge(pre_ready, 1)
            for h in range(2):
                dve.wait_ge(half_done, AT["wo", h] + 1)
                cols = slice(h * HALF, (h + 1) * HALF)
                link(tt(acc[0:N, cols], bank[BANKS["wo"] + h][0:N, :], acc[0:N, cols], ALU.add))
            layernorm_stats(acc, 40, var2_ready)
            dve.wait_ge(std2_ready, 1)
            link(nc.vector.reciprocal(small[0:N, 44:45], small[0:N, 43:44]))
            for h in range(2):
                ts(xn[0:N, h * HALF:(h + 1) * HALF], acc[0:N, h * HALF:(h + 1) * HALF],
                   small[0:N, 40:41], small[0:N, 44:45], ALU.subtract, ALU.mult)\
                    .then_inc(xn2_ready, 1)

            E1, SG, BI, RANK, SEL, W = range(1, 7)
            dve.wait_ge(gate_exp, 1)
            link(ts(route[0:N, E1, :], route[0:N, 0, :], 1.0, None, ALU.add))
            link(nc.vector.reciprocal(route[0:N, SG, :], route[0:N, E1, :]))
            dve.wait_ge(gate_landed, 32)
            link(tt(route[0:N, BI, :], route[0:N, SG, :], ebias[0:N, :], ALU.add))
            others = route[0:N, BI, :].unsqueeze(1).broadcast_to([N, EXPERTS, EXPERTS])
            own = route[0:N, BI, :].unsqueeze(2).broadcast_to([N, EXPERTS, EXPERTS])
            gt = beat[0:N, 0, :].rearrange("n (e o) -> n e o", e=EXPERTS)
            eq = beat[0:N, 1, :].rearrange("n (e o) -> n e o", e=EXPERTS)
            tt(gt, others, own, ALU.is_gt)
            link(tt(eq, others, own, ALU.is_equal))
            link(tt(eq, eq, lower[0:N, :, :], ALU.mult))
            link(tt(gt, gt, eq, ALU.add))
            link(nc.vector.tensor_reduce(route[0:N, RANK, :], gt, AX_X, ALU.add))
            link(ts(route[0:N, SEL, :], route[0:N, RANK, :], 2.0, None, ALU.is_lt))
            tt(route[0:N, W, :], route[0:N, SG, :], route[0:N, SEL, :], ALU.mult)\
                .then_inc(route_ready, 1)

            for j, (t0, t1) in enumerate(TILES):
                dve.wait_ge(relu_done, j + 1)
                r = sh_relu[:, t0 * N:t1 * N]
                tt(sh_h[:, t0 * N:t1 * N], r, r, ALU.mult).then_inc(h_ready, 1)
                if j == 0:
                    for b in range(2):
                        dve.wait_ge(w_all_psum, b + 1)
                        nc.vector.tensor_copy(w_all[:, 4 * b:4 * b + 4, :],
                                              tiles(bank[2 + b][:, 0:GROUP * N]))\
                          .then_inc(free23, 1)
                    dve.wait_ge(free23, 2)
                    tt(tiles(xe[:]), tiles(xnt[:]), w_all[:, 0:1, :].broadcast_to([P, KT, N]),
                       ALU.mult).then_inc(xe_ready, 1)
            for h in range(2):
                dve.wait_ge(down_done, PARTS)
                cols = slice(h * HALF, (h + 1) * HALF)
                tt(acc[0:N, cols], bank[h][0:N, :], acc[0:N, cols], ALU.add)\
                    .then_inc(free01, 1)
            dve.wait_ge(free01, 2)
            nc.vector.tensor_copy(small[:, 60:61], small[:, 28:29]).then_inc(added, 1)
            nc.vector.tensor_copy(small[:, 61:62], small[:, 28:29]).then_inc(added, 1)

            def expert(i, b, last):
                for j, (t0, t1) in enumerate(TILES):
                    dve.wait_ge(relu_done, i * (2 * PARTS) + (PARTS * (b + 1) + j + 1))
                    if j == 0:
                        dve.wait_ge(down_done, i * (2 * PARTS) + PARTS * (b + 1))
                    r = e_relu[:, t0 * N:t1 * N]
                    tt(e_h[:, t0 * N:t1 * N], r, r, ALU.mult).then_inc(h_ready, 1)
                if not last:
                    dve.wait_ge(up_done, i * (2 * PARTS) + PARTS * (b + 2))
                    w = w_all[:, bass.ds(i * 2 + (b + 1), 1), :]
                    tt(tiles(xe[:]), tiles(xnt[:]), w.broadcast_to([P, KT, N]), ALU.mult)\
                        .then_inc(xe_ready, 1)
                for h in range(2):
                    if b:
                        dve.wait_ge(free01, i * 2 + (2 + h + 1))
                    else:
                        dve.wait_ge(free23, i * 2 + (2 + h + 1))
                    dve.wait_ge(added, i * 4 + (2 * (b + 1) + h))
                    cols = slice(h * HALF, (h + 1) * HALF)
                    tt(acc[0:N, cols], rounded[0:N, cols], acc[0:N, cols], ALU.add)\
                        .then_inc(added, 1)

            with dve.Fori(0, EXPERTS // 2 - 1) as i:
                for b in range(2):
                    expert(i, b, False)
            expert(EXPERTS // 2 - 1, 0, False)
            expert(EXPERTS // 2 - 1, 1, True)

        @block.tensor
        def _(pe):
            mm = nc.tensor.matmul
            pe.wait_ge(pool_step, 2)
            pe.wait_ge(key_ready, 1)
            pe.wait_ge(dve_step, 1)
            for r in range(EC // GROUP):
                if r >= 2:
                    pe.wait_ge(key_used, r - 1)
                for g in range(GROUP):
                    c = r * GROUP + g
                    ins = mm(bank[6 + r % 2][:, g * P:(g + 1) * P],
                             ident[0:EC, c:c + 1].broadcast_to([EC, P]), key_r,
                             start=True, stop=True)
                ins.then_inc(key_psum, 1)

            def transpose_rows(src, banks, ready, psum):
                for b in range(2):
                    pe.wait_ge(ready, b + 1)
                    for g in range(GROUP):
                        k = b * GROUP + g
                        ins = nc.tensor.transpose(bank[banks + b][:, g * N:(g + 1) * N],
                                                  src[0:N, k * P:(k + 1) * P], ident[0:N, 0:N])
                    ins.then_inc(psum, 1)

            transpose_rows(xn, 4, xn_ready, xnt_psum)
            pe.wait_ge(xnt_ready, 2)

            def out_transposed(m, h, src):
                c = AT[m, h]
                half_landed(pe, c)
                for o in range(HT):
                    for k in range(KT):
                        ins = mm(bank[BANKS[m] + h][:, o * N:(o + 1) * N],
                                 slots[c % SLOTS][:, k, o * P:(o + 1) * P], tiles(src)[:, k, :],
                                 start=(k == 0), stop=(k == KT - 1))
                ins.then_inc(half_done, 1)

            def out_rows(m, h, src):
                c = AT[m, h]
                half_landed(pe, c)
                for k in range(KT):
                    ins = mm(bank[BANKS[m] + h][0:N, :], tiles(src)[:, k, :],
                             slots[c % SLOTS][:, k, :], start=(k == 0), stop=(k == KT - 1))
                ins.then_inc(half_done, 1)

            for h in range(2):
                out_transposed("wq", h, xnt[:])
            pe.wait_ge(onehot_ready, 1)
            for r in range(5):
                if r >= 2:
                    pe.wait_ge(code_used, r - 1)
                for c in range(5 * r, min(5 * r + 5, EC)):
                    ins = mm(bank[4 + r % 2][0:N, (c - 5 * r) * N:(c - 5 * r + 1) * N],
                             oh_src[:, c, :], oh_dst[:, c, :], start=True, stop=True)
                ins.then_inc(code_psum, 1)
            for h in range(2):
                out_transposed("wk", h, xnt[:])
            for h in range(2):
                pe.wait_ge(half_out, AT["wq", h] + 1)
                out_transposed("wv", h, xnt[:])
            pe.wait_ge(half_out, AT["wq", 1] + 1)
            for h in range(2):
                pe.wait_ge(half_out, AT["wk", h] + 1)
                out_transposed("wiq", h, q1)
            pe.wait_ge(half_out, AT["wk", 1] + 1)
            for h in range(2):
                pe.wait_ge(half_out, AT["wv", h] + 1)
                out_transposed("wik", h, k1)
            pe.wait_ge(half_out, AT["wv", 1] + 1)
            for h in range(2):
                pe.wait_ge(half_out, AT["wiq", h] + 1)
                out_rows("wiv", h, v1)
            pe.wait_ge(half_out, AT["wik", 1] + 1)
            pe.wait_ge(code_used, 5)
            for b in range(2):
                for g in range(GROUP):
                    for odd in range(2):
                        half = slice(DH * odd, DH * (odd + 1))
                        ins = mm(bank[4 + 2 * odd + b][0:N, g * N:(g + 1) * N],
                                 tiles(q2)[half, b * GROUP + g, :],
                                 tiles(k2)[half, b * GROUP + g, :], start=True, stop=True)
                ins.then_inc(scores_psum, 1)
            for h in range(2):
                pe.wait_ge(half_out, AT["wik", h] + 1)
                out_rows("mq", h, xnt[:])
            for h in range(2):
                pe.wait_ge(half_out, AT["wiv", h] + 1)
                out_rows("mk", h, xnt[:])
            pe.wait_ge(attn_ready, 1)
            for b in range(4):
                for g in range(GROUP):
                    at = b * GROUP + g
                    ins = nc.tensor.transpose(bank[4 + b][0:N, g * N:(g + 1) * N],
                                              scores[0:N, at * N:(at + 1) * N], ident[0:N, 0:N])
                ins.then_inc(attn_t_psum, 1)
            pe.wait_ge(relu_q_ready, 2)
            for h in range(2):
                pe.wait_ge(half_out, AT["mq", h] + 1)
                out_rows("mv", h, xnt[:])
            pe.wait_ge(attn_t_ready, 4)
            pe.wait_ge(half_out, AT["wiv", 1] + 1)
            for b in range(2):
                for g in range(2 * GROUP):
                    hd = b * 2 * GROUP + g
                    p0 = DH * (hd % 2)
                    at = PAIR * (hd % 2) + hd // 2
                    ins = mm(bank[4 + b][p0:p0 + DH, (g // 2) * N:(g // 2 + 1) * N],
                             v2[0:N, hd * DH:(hd + 1) * DH], attn_t[0:N, at * N:(at + 1) * N],
                             start=True, stop=True)
                ins.then_inc(pv_psum, 1)
            for b in range(2):
                pe.wait_ge(half_out, AT["mv", b] + 1)
                for g in range(GROUP):
                    k = b * GROUP + g
                    ins = nc.tensor.transpose(bank[6 + b][:, g * N:(g + 1) * N],
                                              mvec[0:N, k * P:(k + 1) * P], ident[0:N, 0:N])
                ins.then_inc(mvec_t_psum, 1)
            pe.wait_ge(out_t_ready, 2)
            out_rows("wo", 0, out_t)
            pe.wait_ge(mvec_t_ready, 2)
            pe.wait_ge(half_out, AT["mk", 1] + 1)
            out_rows("mo", 0, mvec_t)
            out_rows("mo", 1, mvec_t)
            out_rows("wo", 1, out_t)

            pe.wait_ge(pre_ready, 1)
            transpose_rows(xn, 2, xn2_ready, xn2t_psum)
            pe.wait_ge(xn2t_ready, 2)
            pe.wait_ge(gate_landed, 32)
            for k in range(KT):
                ins = mm(bank[7][0:N, 0:EXPERTS], tiles(xnt[:])[:, k, :],
                         gate[:, k * EXPERTS:(k + 1) * EXPERTS], start=(k == 0), stop=(k == KT - 1))
            ins.then_inc(logits_psum, 1)
            for j, (t0, t1) in enumerate(TILES):
                pe.wait_ge(shared_landed[j], 16)
                for t in range(t0, t1):
                    for k in range(KT):
                        ins = mm(bank[4 + j][:, (t - t0) * N:(t - t0 + 1) * N], sh_up_t[:, t, k, :],
                                 tiles(xnt[:])[:, k, :], start=(k == 0), stop=(k == KT - 1))
                ins.then_inc(up_done, 1)
                if j == 0:
                    pe.wait_ge(route_ready, 1)
                    for b in range(2):
                        for g in range(GROUP):
                            e = b * GROUP + g
                            ins = mm(bank[2 + b][:, g * N:(g + 1) * N],
                                     route[0:N, 6, e:e + 1].broadcast_to([N, P]), ident[0:N, 0:N],
                                     start=True, stop=True)
                        ins.then_inc(w_all_psum, 1)
            for j, (t0, t1) in enumerate(SH_DN_TILES):
                pe.wait_ge(shared_landed[PARTS + j], 16)
                pe.wait_ge(h_ready, [1, 2, 3][j])
                for t in range(t0, t1):
                    for h in range(2):
                        w = sh_dn[j][:, (t - t0) * UNIT + h * HALF:(t - t0) * UNIT + (h + 1) * HALF]
                        ins = mm(bank[h][0:N, :], tiles(sh_h)[:, t, :], w,
                                 start=(t == 0), stop=(t == TT - 1))
                ins.then_inc(down_done, 1)

            def expert(i, b):
                up = stage[b][:, 0:TT * UNIT // 2].bitcast(BF16)\
                    .rearrange("p (t k j) -> p t k j", t=TT, k=KT)
                down = stage[b][:, TT * UNIT // 2:TT * UNIT].bitcast(BF16)
                pe.wait_ge(xe_ready, i * 2 + (b + 1))
                for j, (t0, t1) in enumerate(TILES):
                    pe.wait_ge(stage_landed[b][j], i * 16 + 16)
                    pe.wait_ge(relu_done, i * (2 * PARTS) + (PARTS * b + j + 1))
                    for t in range(t0, t1):
                        for k in range(KT):
                            ins = mm(bank[4 + j][:, (t - t0) * N:(t - t0 + 1) * N], up[:, t, k, :],
                                     tiles(xe[:])[:, k, :], start=(k == 0), stop=(k == KT - 1))
                    ins.then_inc(up_done, 1)
                pe.wait_ge(free01 if b else free23, i * 2 + 2)
                for j, (t0, t1) in enumerate(TILES):
                    pe.wait_ge(stage_landed[b][PARTS + j], i * 16 + 16)
                    pe.wait_ge(h_ready, i * (2 * PARTS) + (PARTS * (b + 1) + j + 1))
                    for t in range(t0, t1):
                        for h in range(2):
                            at = t * UNIT + h * HALF
                            ins = mm(bank[2 * (1 - b) + h][0:N, :], tiles(e_h)[:, t, :],
                                     down[:, at:at + HALF], start=(t == 0), stop=(t == TT - 1))
                    ins.then_inc(down_done, 1)

            with pe.Fori(0, EXPERTS // 2) as i:
                for b in range(2):
                    expert(i, b)


def kernel(**inputs):
    import numpy as np
    import concourse.bacc as bacc
    from concourse import mybir as mb
    from concourse.bass_utils import run_bass_kernel_spmd

    def tiled_rows(w):
        return w.reshape(KT, P, 2, HALF).transpose(2, 1, 0, 3).reshape(2, P, SLOT)

    g = {k: np.asarray(v) for k, v in inputs.items()}
    wkv = g["L0_mix_Wkv"]
    mats = {
        "wq": g["L0_gnn_wq"].T, "wk": g["L0_gnn_wk"].T, "wv": g["L0_gnn_wv"].T,
        "wiq": g["L0_gnn_wiq"].T, "wik": g["L0_gnn_wik"].T, "wiv": g["L0_gnn_wiv"].T,
        "mq": g["L0_mix_Wq"], "mk": wkv[:, :D], "mv": wkv[:, D:],
        "mo": g["L0_mix_Wo"], "wo": g["L0_gnn_wo"].T,
    }
    arrays = {"x": g["x"]}
    for name, w in mats.items():
        arrays[f"mat_{name}"] = tiled_rows(w)
    arrays["bias_cols"] = np.stack([g[f"L0_gnn_{b}"].reshape(KT, P).T
                                    for b in ("bq", "bk", "bv", "biq", "bik")], axis=1)\
        .reshape(P, len(BIASES) * KT)
    arrays["bias_v"] = g["L0_gnn_biv"].reshape(1, D)
    arrays["bias_o"] = g["L0_gnn_bo"].reshape(1, D)
    arrays["ln_gamma"] = g["L0_mix_ln_gamma"].reshape(1, D)
    arrays["ln_beta"] = g["L0_mix_ln_beta"].reshape(1, D)
    arrays["src_rows"] = g["src"].reshape(EC, P)
    arrays["dst_rows"] = g["dst"].reshape(EC, P)
    arrays["src_cols"] = g["src"].reshape(EC, P).T
    arrays["dst_cols"] = g["dst"].reshape(EC, P).T
    arrays["type_cols"] = g["edge_type_5"].reshape(EC, P).T
    arrays["edge_w"] = g["L0_gnn_edge_type_weights"].reshape(1, ETYPES)
    arrays["gate_w"] = g["L0_ffn_gate_w"].reshape(EXPERTS, KT, P).transpose(2, 1, 0).reshape(P, KT * EXPERTS)
    arrays["expert_bias"] = g["L0_ffn_expert_bias"].reshape(1, EXPERTS)
    arrays["shared_up"] = g["L0_ffn_shared_w_up"].reshape(TT, P, KT, P).transpose(3, 0, 2, 1)\
        .reshape(P, TT * UNIT)
    arrays["shared_down"] = g["L0_ffn_shared_w_down"].reshape(D, TT, P).transpose(2, 1, 0)\
        .reshape(P, TT * UNIT)
    arrays["expert_up"] = g["L0_ffn_w_up"].reshape(EXPERTS, TT, P, KT, P).transpose(0, 4, 1, 3, 2)\
        .reshape(EXPERTS, P, TT * UNIT)
    arrays["expert_down"] = g["L0_ffn_w_down"].reshape(EXPERTS, D, TT, P).transpose(0, 3, 2, 1)\
        .reshape(EXPERTS, P, TT * UNIT)
    arrays = {f"in_{k}": np.ascontiguousarray(v) for k, v in arrays.items()}

    nc = bacc.Bacc("TRN2", target_bir_lowering=False, num_devices=1)
    aps = {k[3:]: nc.dram_tensor(k, a.shape, mb.dt.from_np(a.dtype), kind="ExternalInput").ap()
           for k, a in arrays.items()}
    out = nc.dram_tensor("out", (N, D), mb.dt.float32, kind="ExternalOutput").ap()
    mat_aps = {k[4:]: aps.pop(k) for k in list(aps) if k.startswith("mat_")}
    gps_layer(nc, mats=mat_aps, out=out, **aps)
    r = run_bass_kernel_spmd(nc, [arrays], core_ids=[0])
    return r.results[0]["out"]
```

```python
from contextlib import ExitStack

import concourse.bass as bass
from concourse import mybir

F32 = mybir.dt.float32
BF16 = mybir.dt.bfloat16
I32 = mybir.dt.int32
ALU = mybir.AluOpType
ACT = mybir.ActivationFunctionType
AX_X = mybir.AxisListType.X

P = 128
N = 96
D = 1024
KT = D // P
HALF = D // 2
HT = HALF // P
H = 16
DH = D // H
PAIR = H // 2
EDGES = 3072
EC = EDGES // P
ETYPES = 4
HID = 1408
TT = HID // P
EXPERTS = 8
EPS = 1e-5
SCALE = 1.0 / DH ** 0.5
ROLL = 3
FEAT = 2 * DH
ABSENT = 1.0e30

GROUP = 4
SLOT = KT * HALF
SLOTS = 5
UNIT = D
TILES = [(0, 4), (4, 8), (8, 11)]
PARTS = len(TILES)

MATS = ["wq", "wk", "wv", "wiq", "wik", "wiv", "mq", "mk", "mv"]
STEPS = [(m, h) for m in MATS for h in range(2)] + [("wo", 0), ("mo", 0), ("mo", 1), ("wo", 1)]
AT = {s: c for c, s in enumerate(STEPS)}
BANKS = {m: 2 * (i % 2) for i, m in enumerate(MATS)} | {"wo": 0, "mo": 2}
KEY_BANKS = [6, 7, 2, 3, 6, 7]
BIASES = ["wq", "wk", "wv", "wiq", "wik"]


def gps_layer(nc, x, mats, bias_cols, bias_v, bias_o, ln_gamma, ln_beta, edge_rows, edge_cols,
              edge_w, gate_w, expert_bias, shared_up, shared_down, expert_up, expert_down, out):
    ctx = ExitStack()
    with ctx:
        def sb(name, shape, dt):
            return ctx.enter_context(nc.sbuf_tensor(name, shape, dt))

        def sem(name):
            return ctx.enter_context(nc.semaphore(name))

        bank = [ctx.enter_context(nc.psum_tensor(f"bank{i}", [P, 512], F32)) for i in range(8)]

        ring = sb("ring", [P, 2 * TT * UNIT], F32)
        stage = [sb(f"stage{b}", [P, TT * UNIT], F32)[:, :] for b in range(2)]
        slots = [ring[:, s * SLOT:(s + 1) * SLOT].rearrange("p (k n) -> p k n", k=KT)
                 for s in range(SLOTS)]
        tail = SLOTS * SLOT
        gamma = ring[:, tail:tail + D]
        beta = ring[:, tail + D:tail + 2 * D]
        sh_up = ring[:, 2 * SLOT:2 * SLOT + TT * UNIT]
        stage.append(sh_up)
        sh_up_t = sh_up.rearrange("p (t k j) -> p t k j", t=TT, k=KT)
        end = 2 * SLOT + TT * UNIT
        sh_dn = [ring[:, end:end + 3 * UNIT], ring[:, 0:4 * UNIT], ring[:, 4 * UNIT:8 * UNIT]]
        SH_DN_TILES = [(0, 3), (3, 7), (7, 11)]

        arena = stage[1]

        def take(at, n):
            return arena[:, at:at + n]

        scores = take(0, H * N)
        attn_t = take(1536, H * N)
        q1 = take(3072, KT * N)
        k1 = take(3840, KT * N)
        v1 = take(4608, KT * N)
        q2 = take(5376, KT * N)
        k2 = take(6144, KT * N)
        v2 = take(6912, D)
        prod = take(7936, H * (FEAT + ROLL))
        relu_q = take(10032, D)
        rolled = take(3072, H * FEAT)
        neg_q = take(5376, D)
        mvec = take(7936, D)
        mvec_t = take(10032, KT * N)
        out_t = take(5632, KT * N)
        bias_v_b = take(10032, D)
        oh_src = take(1536, EC * N // 2).bitcast(BF16).rearrange("p (c s) -> p c s", c=EC)
        oh_dst = take(7936, EC * N // 2).bitcast(BF16).rearrange("p (c s) -> p c s", c=EC)
        same = take(0, P)

        def tiles(ap):
            return ap.rearrange("p (k n) -> p k n", n=N)

        xs = sb("xs", [P, TT * N], F32)
        xn = sb("xn", [P, D], F32)
        xnt = sb("xnt", [P, KT * N], F32)
        acc = sb("acc", [P, D], F32)
        hbuf = sb("hbuf", [P, TT * N], F32)
        xe = sb("xe", [P, KT * N], BF16)
        rounded = sb("rounded", [P, D], BF16)
        w_all = sb("w_all", [P, EXPERTS, N], F32)
        bias_o_b = hbuf[:, 0:D]
        sh_h = xs[:, :]
        sh_relu = hbuf[:, :]
        e_h = hbuf[:, 0:TT * N // 2].bitcast(BF16)
        e_relu = xn[:, 0:TT * N // 2].bitcast(BF16)

        ident = sb("ident", [P, P], F32)
        lower = sb("lower", [P, EXPERTS, EXPERTS], F32)
        iota_i = sb("iota_i", [P, N], I32)
        iota = sb("iota", [P, N], F32)
        codebase_i = sb("codebase_i", [P, EC], I32)
        bias_c = sb("bias_c", [P, len(BIASES) * KT], F32)
        gate = sb("gate", [P, KT * EXPERTS], F32)
        ebias = sb("ebias", [P, EXPERTS], F32)
        ew = sb("ew", [P, ETYPES], F32)
        later = acc[:, 0:P]
        edge_r = acc[0:EC, P:3 * P].bitcast(I32)
        ends_r = acc[0:EC, 3 * P:4 * P].bitcast(BF16)
        edge_c = acc[:, 4 * P:4 * P + 3 * EC].bitcast(I32).rearrange("p (r c) -> p r c", r=3)
        pick = acc[0:EC, 5 * P:5 * P + EC].bitcast(BF16)
        edge_f = acc[:, 6 * P:6 * P + 8 * EC].rearrange("p (r c) -> p r c", r=8)
        code = hbuf[:, 0:2 * N].rearrange("p (r n) -> p r n", r=2)
        mtmp = hbuf[:, 2 * N:4 * N].rearrange("p (r n) -> p r n", r=2)
        code_i = hbuf[:, 4 * N:5 * N].bitcast(I32)
        mask = sb("mask", [P, N], F32)
        small = sb("small", [P, 64], F32)
        stat = sb("stat", [P, 2, 6], F32)
        head = sb("head", [P, 6, H], F32)
        route = sb("route", [P, 8, EXPERTS], F32)
        beat = sb("beat", [P, 2, EXPERTS * EXPERTS], F32)

        x_landed = sem("x_landed")
        rows_landed = sem("rows_landed")
        cols_landed = sem("cols_landed")
        ew_landed = sem("ew_landed")
        bias_landed = sem("bias_landed")
        bias_v_landed = sem("bias_v_landed")
        ln_landed = sem("ln_landed")
        bias_o_landed = sem("bias_o_landed")
        gate_landed = sem("gate_landed")
        first_landed = sem("first_landed")
        slot_landed = [sem(f"slot_landed{s}") for s in range(SLOTS)]
        shared_landed = [sem(f"shared_landed{j}") for j in range(2 * PARTS)]
        stage_landed = [[sem(f"stage_landed{b}_{j}") for j in range(2 * PARTS)] for b in range(3)]
        out_landed = sem("out_landed")
        pool_step = sem("pool_step")
        spread = sem("spread")
        dve_step = sem("dve_step")
        act_step = sem("act_step")
        ends_ready = sem("ends_ready")
        one_ready = sem("one_ready")
        key_psum = sem("key_psum")
        key_used = sem("key_used")
        onehot_ready = sem("onehot_ready")
        code_psum = sem("code_psum")
        code_used = sem("code_used")
        soft_in = sem("soft_in")
        soft_log = sem("soft_log")
        var1_ready = sem("var1_ready")
        std1_ready = sem("std1_ready")
        xn_ready = sem("xn_ready")
        xnt_psum = sem("xnt_psum")
        xnt_ready = sem("xnt_ready")
        half_done = sem("half_done")
        half_out = sem("half_out")
        scores_psum = sem("scores_psum")
        shifted = sem("shifted")
        exps_ready = sem("exps_ready")
        attn_ready = sem("attn_ready")
        attn_t_psum = sem("attn_t_psum")
        attn_t_ready = sem("attn_t_ready")
        pv_psum = sem("pv_psum")
        out_t_ready = sem("out_t_ready")
        relu_q_ready = sem("relu_q_ready")
        prod_ready = sem("prod_ready")
        mvec_ready = sem("mvec_ready")
        mvec_t_psum = sem("mvec_t_psum")
        mvec_t_ready = sem("mvec_t_ready")
        varm_ready = sem("varm_ready")
        stdm_ready = sem("stdm_ready")
        pre_ready = sem("pre_ready")
        var2_ready = sem("var2_ready")
        std2_ready = sem("std2_ready")
        xn2_ready = sem("xn2_ready")
        xn2t_psum = sem("xn2t_psum")
        xn2t_ready = sem("xn2t_ready")
        logits_psum = sem("logits_psum")
        gate_exp = sem("gate_exp")
        route_ready = sem("route_ready")
        w_all_psum = sem("w_all_psum")
        w_all_ready = sem("w_all_ready")
        xe_ready = sem("xe_ready")
        up_done = sem("up_done")
        relu_done = sem("relu_done")
        h_ready = sem("h_ready")
        down_done = sem("down_done")
        down_first = sem("down_first")
        out_taken = sem("out_taken")
        added = sem("added")

        def up_before(e):
            return (1, 1 + PARTS)[e] if isinstance(e, int) and e < 2 else e * PARTS + PARTS

        def down_before(e):
            return (0, PARTS)[e] if isinstance(e, int) and e < 2 else e * PARTS + PARTS

        block = ctx.enter_context(nc.Block())

        def half_landed(eng, c):
            eng.wait_ge(slot_landed[c % SLOTS], 16 * (c // SLOTS + 1))

        @block.sync
        def _(sp):
            sp.dma_start(xs[0:N, 0:D], x).then_inc(x_landed, 16)
            sp.dma_start(edge_r, edge_rows).then_inc(rows_landed, 16)
            sp.dma_start(edge_c, edge_cols).then_inc(cols_landed, 16)
            for c, (m, h) in enumerate(STEPS):
                if c >= SLOTS:
                    sp.wait_ge(half_done, c - SLOTS + 1)
                if c == 0:
                    src = mats[m][h].rearrange("p (k n) -> p k n", k=KT)
                    for part, landed in enumerate((first_landed, slot_landed[0])):
                        cols = slice(part * 2 * P, (part + 1) * 2 * P)
                        sp.dma_start(slots[0][:, :, cols], src[:, :, cols]).then_inc(landed, 16)
                    sp.dma_start(bias_c[:], bias_cols).then_inc(bias_landed, 16)
                    sp.dma_start(ew[:, :], edge_w.broadcast_to([P, ETYPES])).then_inc(ew_landed, 16)
                    continue
                dst = ring[:, (c % SLOTS) * SLOT:(c % SLOTS + 1) * SLOT]
                sp.dma_start(dst, mats[m][h]).then_inc(slot_landed[c % SLOTS], 16)
            last = {c % SLOTS: c for c in range(len(STEPS))}
            for j, (t0, t1) in enumerate(TILES):
                sp.wait_ge(half_done, last[2 + j] + 1)
                sp.dma_start(sh_up[:, t0 * UNIT:t1 * UNIT], shared_up[:, t0 * UNIT:t1 * UNIT])\
                  .then_inc(shared_landed[j], 16)
            for j, (t0, t1) in enumerate(SH_DN_TILES):
                if j == 0:
                    sp.wait_ge(pre_ready, 1)
                else:
                    sp.wait_ge(half_done, last[j - 1] + 1)
                sp.dma_start(sh_dn[j], shared_down[:, t0 * UNIT:t1 * UNIT])\
                  .then_inc(shared_landed[PARTS + j], 16)
            for h in range(2):
                sp.wait_ge(added, 2 * EXPERTS + 1 + h)
                sp.dma_start(out[:, h * HALF:(h + 1) * HALF], acc[0:N, h * HALF:(h + 1) * HALF])\
                  .then_inc(out_landed, 16)
            sp.wait_ge(out_landed, 32)

        @block.gpsimd
        def _(pool):
            nc.gpsimd.memset(ident[:], 0.0).then_inc(pool_step, 1)
            pool.wait_ge(pool_step, 1)
            nc.gpsimd.affine_select(out=ident[:], in_=ident[:], compare_op=ALU.not_equal, fill=1.0,
                                    base=0, pattern=[[-1, P]], channel_multiplier=1)\
              .then_inc(pool_step, 1)
            nc.gpsimd.memset(later, 1.0).then_inc(pool_step, 1)
            pool.wait_ge(pool_step, 3)
            nc.gpsimd.affine_select(out=later, in_=later, compare_op=ALU.is_gt, fill=0.0,
                                    base=0, pattern=[[1, P]], channel_multiplier=-1)\
              .then_inc(pool_step, 1)
            nc.gpsimd.iota(iota_i[:], pattern=[[1, N]], base=0, channel_multiplier=0)\
              .then_inc(pool_step, 1)
            nc.gpsimd.iota(codebase_i[:], pattern=[[ETYPES, EC]], base=0, channel_multiplier=0)\
              .then_inc(pool_step, 1)
            nc.gpsimd.memset(lower[:], 1.0).then_inc(pool_step, 1)
            pool.wait_ge(pool_step, 7)
            nc.gpsimd.affine_select(out=lower[:], in_=lower[:], compare_op=ALU.is_gt, fill=0.0,
                                    base=0, pattern=[[1, EXPERTS], [-1, EXPERTS]],
                                    channel_multiplier=0).then_inc(pool_step, 1)
            pool.wait_ge(bias_v_landed, 16)
            nc.gpsimd.partition_broadcast(bias_v_b, bias_v_b[0:1, :]).then_inc(spread, 1)
            pool.wait_ge(ln_landed, 32)
            nc.gpsimd.partition_broadcast(gamma, gamma[0:1, :]).then_inc(spread, 1)
            nc.gpsimd.partition_broadcast(beta, beta[0:1, :]).then_inc(spread, 1)

            def load(e, b, m, j):
                t0, t1 = TILES[j]
                place = stage[b].rearrange("p (m n) -> p m n", m=2)[:, m, :].bitcast(BF16)
                src = (expert_up, expert_down)[m][bass.ds(e, 1), :, t0 * UNIT:t1 * UNIT]
                pool.dma_start(place[:, t0 * UNIT:t1 * UNIT], src.rearrange("a p n -> (a p) n"))\
                    .then_inc(stage_landed[b][PARTS * m + j], 16)

            for m in range(2):
                for j in range(PARTS):
                    pool.wait_ge(half_done, 4 + 2 * (PARTS * m + j))
                    load(0, 0, m, j)
            pool.wait_ge(bias_o_landed, 16)
            nc.gpsimd.partition_broadcast(bias_o_b, bias_o_b[0:1, :]).then_inc(spread, 1)
            pool.wait_ge(pv_psum, 2)
            pool.wait_ge(mvec_t_psum, 2)
            for j in range(PARTS):
                load(1, 1, 0, j)
            load(1, 1, 1, 1)
            pool.wait_ge(half_done, AT["mo", 1] + 1)
            load(1, 1, 1, 2)
            pool.wait_ge(half_done, len(STEPS))
            load(1, 1, 1, 0)
            def place_free(n, m, j):
                before = (up_before, down_before)[m]
                second = before(2 + n) + j + 1
                if n < 2:
                    return before(n) + j + 1, second
                return (2 * PARTS + (2 if j == 0 else 3), 2 * PARTS + 1)[m], second

            with pool.Fori(0, 2) as i:
                for n in range(3):
                    for m, done in enumerate((up_done, down_done)):
                        for j in range(PARTS):
                            first, second = place_free(n, m, j)
                            count = pool.to_reg(i * (second - first) + first)
                            pool.wait_ge(pre_ready, 1)
                            pool.wait_ge(done, count)
                            load(i * 3 + (2 + n), n, m, j)

        @block.scalar
        def _(act):
            act.wait_ge(var1_ready, 1)
            nc.scalar.activation(small[0:N, 3:4], small[0:N, 2:3], ACT.Sqrt).then_inc(std1_ready, 1)
            act.dma_start(bias_v_b[0:1, :], bias_v).then_inc(bias_v_landed, 16)
            act.dma_start(gamma[0:1, :], ln_gamma).then_inc(ln_landed, 16)
            act.dma_start(beta[0:1, :], ln_beta).then_inc(ln_landed, 16)
            act.dma_start(gate[:], gate_w).then_inc(gate_landed, 16)
            act.dma_start(ebias[:], expert_bias.broadcast_to([P, EXPERTS])).then_inc(gate_landed, 16)
            for b in range(2):
                act.wait_ge(xnt_psum, b + 1)
                nc.scalar.activation(xnt[:, b * GROUP * N:(b + 1) * GROUP * N],
                                     bank[4 + b][:, 0:GROUP * N], ACT.Copy).then_inc(xnt_ready, 1)
            act.wait_ge(soft_in, 1)
            nc.scalar.activation(small[:, 20:24], small[:, 16:20], ACT.Exp, scale=-1.0)\
              .then_inc(act_step, 1)
            act.wait_ge(act_step, 1)
            act.wait_ge(one_ready, 1)
            nc.scalar.activation(small[:, 24:28], small[:, 20:24], ACT.Ln, bias=small[:, 28:29])\
              .then_inc(soft_log, 1)
            act.wait_ge(shifted, 1)
            act.dma_start(bias_o_b[0:1, :], bias_o).then_inc(bias_o_landed, 16)
            nc.scalar.activation(scores[0:N, :], scores[0:N, :], ACT.Exp).then_inc(exps_ready, 1)
            for h in range(2):
                act.wait_ge(half_done, AT["mq", h] + 1)
                if h == 0:
                    act.wait_ge(half_out, AT["wiv", 1] + 1)
                nc.scalar.activation(relu_q[0:N, h * HALF:(h + 1) * HALF],
                                     bank[BANKS["mq"] + h][0:N, :], ACT.Relu).then_inc(relu_q_ready, 1)
            for b in range(4):
                act.wait_ge(attn_t_psum, b + 1)
                nc.scalar.activation(attn_t[0:N, b * GROUP * N:(b + 1) * GROUP * N],
                                     bank[4 + b][0:N, 0:GROUP * N], ACT.Copy)\
                  .then_inc(attn_t_ready, 1)
            act.wait_ge(prod_ready, 1)
            for b in range(2):
                act.wait_ge(pv_psum, b + 1)
                nc.scalar.activation(out_t[:, b * GROUP * N:(b + 1) * GROUP * N],
                                     bank[4 + b][:, 0:GROUP * N], ACT.Copy)\
                  .then_inc(out_t_ready, 1)
            for b in range(2):
                act.wait_ge(mvec_t_psum, b + 1)
                nc.scalar.activation(mvec_t[:, b * GROUP * N:(b + 1) * GROUP * N],
                                     bank[6 + b][:, 0:GROUP * N], ACT.Copy)\
                  .then_inc(mvec_t_ready, 1)
            act.wait_ge(varm_ready, 1)
            nc.scalar.activation(small[0:N, 35:36], small[0:N, 34:35], ACT.Sqrt).then_inc(stdm_ready, 1)
            act.wait_ge(var2_ready, 1)
            nc.scalar.activation(small[0:N, 43:44], small[0:N, 42:43], ACT.Sqrt).then_inc(std2_ready, 1)
            for b in range(2):
                act.wait_ge(xn2t_psum, b + 1)
                nc.scalar.activation(xnt[:, b * GROUP * N:(b + 1) * GROUP * N],
                                     bank[2 + b][:, 0:GROUP * N], ACT.Copy).then_inc(xn2t_ready, 1)
            act.wait_ge(logits_psum, 1)
            nc.scalar.activation(route[0:N, 0, :], bank[7][0:N, 0:EXPERTS], ACT.Exp, scale=-1.0)\
              .then_inc(gate_exp, 1)
            def shared_relu(j, done):
                t0, t1 = TILES[j]
                act.wait_ge(up_done, done)
                nc.scalar.activation(sh_relu[:, t0 * N:t1 * N], bank[4 + j][:, 0:(t1 - t0) * N],
                                     ACT.Relu).then_inc(relu_done, 1)

            def expert(e):
                up0, down0 = up_before(e), down_before(e)
                for j, (t0, t1) in enumerate(TILES):
                    act.wait_ge(up_done, up0 + (j + 1))
                    if j == 0:
                        act.wait_ge(h_ready, up0)
                    nc.scalar.activation(e_relu[:, t0 * N:t1 * N], bank[4 + j][:, 0:(t1 - t0) * N],
                                         ACT.Relu).then_inc(relu_done, 1)
                if not isinstance(e, int):
                    act.wait_ge(added, e * 2 + 2)
                elif e:
                    act.wait_ge(added, 2 * e)
                for h in range(2):
                    if h == 0:
                        act.wait_ge(down_first, e + 1)
                    else:
                        act.wait_ge(down_done, down0 + PARTS)
                    nc.scalar.activation(rounded[0:N, h * HALF:(h + 1) * HALF],
                                         bank[h][0:N, :], ACT.Copy).then_inc(out_taken, 1)

            shared_relu(0, 1)
            expert(0)
            expert(1)
            act.wait_ge(down_done, 2 * PARTS)
            for j in (1, 2):
                shared_relu(j, 2 * PARTS + j + 1)
            with act.Fori(2, EXPERTS) as e:
                expert(e)

        @block.vector
        def _(dve):
            chain = [0]

            def link(ins):
                chain[0] += 1
                ins.then_inc(dve_step, 1)
                dve.wait_ge(dve_step, chain[0])

            tt, ts, stt = nc.vector.tensor_tensor, nc.vector.tensor_scalar, nc.vector.scalar_tensor_tensor

            def layernorm_stats(src, at, ready):
                for h in range(2):
                    ins = nc.vector.bn_stats(stat[0:N, h, :], src[0:N, h * HALF:(h + 1) * HALF])
                    if h == 1:
                        link(ins)
                link(nc.vector.bn_aggr(small[0:N, at:at + 2], stat[0:N, :, :]))
                ts(small[0:N, at + 2:at + 3], small[0:N, at + 1:at + 2], EPS, None, ALU.add)\
                    .then_inc(ready, 1)

            dve.wait_ge(pool_step, 2)
            ts(pick[:, 0:EC], ident[0:EC, 0:EC], float(N), None, ALU.mult).then_inc(ends_ready, 1)
            nc.vector.tensor_copy(pick[:, EC:2 * EC], ident[0:EC, 0:EC]).then_inc(ends_ready, 1)
            dve.wait_ge(x_landed, 16)
            layernorm_stats(xs, 0, var1_ready)
            dve.wait_ge(rows_landed, 16)
            nc.vector.tensor_copy(ends_r, edge_r).then_inc(ends_ready, 1)
            nc.vector.memset(small[:, 28:29], 1.0).then_inc(one_ready, 1)
            dve.wait_ge(cols_landed, 16)
            SRC, DST, TYP, KEY, LAST, VAL, TMP, BASE = range(8)
            link(nc.vector.tensor_copy(edge_f[:, SRC:TYP + 1, :], edge_c[:, :, :]))
            dve.wait_ge(std1_ready, 1)
            link(nc.vector.reciprocal(small[0:N, 4:5], small[0:N, 3:4]))
            for h in range(2):
                ts(xn[0:N, h * HALF:(h + 1) * HALF], xs[0:N, h * HALF:(h + 1) * HALF], small[0:N, 0:1],
                   small[0:N, 4:5], ALU.subtract, ALU.mult).then_inc(xn_ready, 1)
            link(stt(edge_f[:, KEY, :], edge_f[:, SRC, :], float(N), edge_f[:, DST, :],
                     ALU.mult, ALU.add))
            dve.wait_ge(ew_landed, 16)
            link(ts(small[:, 12:16], ew[:], -1.0, None, ALU.mult))
            tt(small[:, 16:20], ew[:], small[:, 12:16], ALU.max).then_inc(soft_in, 1)
            dve.wait_ge(pool_step, 8)
            for r in range(EC // GROUP):
                dve.wait_ge(key_psum, r + 1)
                if r:
                    dve.wait_ge(key_used, r)
                for g in range(GROUP):
                    c = r * GROUP + g
                    ins = stt(same, bank[KEY_BANKS[r]][:, g * P:(g + 1) * P],
                              edge_f[:, KEY, c:c + 1], later, ALU.is_equal, ALU.mult,
                              accum_out=edge_f[:, LAST, c:c + 1])
                    if g == GROUP - 1:
                        ins.then_inc(key_used, 1)
                    else:
                        link(ins)
            dve.wait_ge(key_used, EC // GROUP)
            link(ts(edge_f[:, LAST, :], edge_f[:, LAST, :], 0.0, None, ALU.is_equal))
            link(ts(edge_f[:, TMP, :], edge_f[:, TYP, :], 0.0, float(ETYPES), ALU.is_equal, ALU.mult))
            link(tt(edge_f[:, VAL, :], edge_f[:, TMP, :], edge_f[:, TYP, :], ALU.add))
            nc.vector.tensor_copy(iota[:], iota_i[:])
            link(nc.vector.tensor_copy(edge_f[:, BASE, :], codebase_i[:]))
            link(tt(edge_f[:, VAL, :], edge_f[:, VAL, :], edge_f[:, BASE, :], ALU.add))
            link(tt(edge_f[:, VAL, :], edge_f[:, VAL, :], edge_f[:, LAST, :], ALU.mult))

            def by_node(row):
                return edge_f[:, row, :].unsqueeze(2).broadcast_to([P, EC, N])

            iota_b = iota[:].unsqueeze(1).broadcast_to([P, EC, N])
            link(tt(oh_dst, iota_b, by_node(DST), ALU.is_equal))
            link(tt(oh_src, iota_b, by_node(SRC), ALU.is_equal))
            tt(oh_src, oh_src, by_node(VAL), ALU.mult).then_inc(onehot_ready, 1)

            def take_t(m, h, dst):
                c = AT[m, h]
                dve.wait_ge(half_done, c + 1)
                at = BIASES.index(m) * KT + h * HT
                b = bias_c[:, at:at + HT].unsqueeze(2).broadcast_to([P, HT, N])
                tt(tiles(dst)[:, h * HT:(h + 1) * HT, :],
                   tiles(bank[BANKS[m] + h][:, 0:HT * N]), b, ALU.add).then_inc(half_out, 1)

            dve.wait_ge(bias_landed, 16)
            for m, dst in (("wq", q1), ("wk", k1), ("wv", v1)):
                for h in range(2):
                    take_t(m, h, dst)

            def codes(r):
                c0, c1 = 5 * r, min(5 * r + 5, EC)
                dve.wait_ge(code_psum, r + 1)
                v = bank[4 + r % 4][0:N, 0:(c1 - c0) * N].rearrange("s (c d) -> s d c", d=N)
                nc.vector.tensor_reduce(code[0:N, 1 if r else 0, :], v, AX_X, ALU.max)\
                    .then_inc(code_used, 1)
                if r:
                    dve.wait_ge(code_used, r + 1)
                    link(tt(code[0:N, 0, :], code[0:N, 0, :], code[0:N, 1, :], ALU.max))

            for r in range(5):
                codes(r)
            link(ts(mtmp[0:N, 0, :], code[0:N, 0, :], 0.0, None, ALU.is_gt))
            link(ts(code_i[0:N, :], code[0:N, 0, :], float(ETYPES - 1), None, ALU.add))
            link(ts(code_i[0:N, :], code_i[0:N, :], ETYPES - 1, None, ALU.bitwise_and))
            link(nc.vector.tensor_copy(code[0:N, 1, :], code_i[0:N, :]))
            dve.wait_ge(soft_log, 1)
            link(ts(small[:, 12:16], ew[:], 0.0, None, ALU.max))
            link(tt(small[:, 12:16], small[:, 12:16], small[:, 24:28], ALU.add))
            for k in range(ETYPES):
                w = small[0:N, 12 + k:13 + k]
                if k == 0:
                    link(ts(mask[0:N, :], code[0:N, 1, :], float(k), w, ALU.is_equal, ALU.mult))
                else:
                    link(ts(mtmp[0:N, 1, :], code[0:N, 1, :], float(k), w, ALU.is_equal, ALU.mult))
                    link(tt(mask[0:N, :], mask[0:N, :], mtmp[0:N, 1, :], ALU.add))
            link(tt(mask[0:N, :], mask[0:N, :], mtmp[0:N, 0, :], ALU.mult))
            link(ts(mtmp[0:N, 1, :], ident[0:N, 0:N], 1.0, ABSENT, ALU.subtract, ALU.mult))
            link(stt(mtmp[0:N, 1, :], ident[0:N, 0:N], small[0:N, 15:16], mtmp[0:N, 1, :],
                     ALU.mult, ALU.add))
            link(ts(mtmp[0:N, 0, :], mtmp[0:N, 0, :], -1.0, 1.0, ALU.mult, ALU.add))
            link(tt(mtmp[0:N, 1, :], mtmp[0:N, 1, :], mtmp[0:N, 0, :], ALU.mult))
            link(tt(mask[0:N, :], mask[0:N, :], mtmp[0:N, 1, :], ALU.add))

            for m, dst in (("wiq", q2), ("wik", k2)):
                for h in range(2):
                    take_t(m, h, dst)
            dve.wait_ge(spread, 1)
            for h in range(2):
                dve.wait_ge(half_done, AT["wiv", h] + 1)
                cols = slice(h * HALF, (h + 1) * HALF)
                tt(v2[0:N, cols], bank[BANKS["wiv"] + h][0:N, :], bias_v_b[0:N, cols], ALU.add)\
                    .then_inc(half_out, 1)

            sc = tiles(scores[0:N, :])
            for b in (0, 2, 1, 3):
                dve.wait_ge(scores_psum, b % 2 + 1)
                ins = stt(sc[:, b * GROUP:(b + 1) * GROUP, :], tiles(bank[4 + b][0:N, 0:GROUP * N]),
                          SCALE, mask[0:N, :].unsqueeze(1).broadcast_to([N, GROUP, N]),
                          ALU.mult, ALU.add)
                link(ins)
            MX, SUM, INV = range(3)

            def by_head(row, n):
                return head[0:N, row, :].unsqueeze(2).broadcast_to([N, H, n])

            link(nc.vector.tensor_reduce(head[0:N, MX, :], sc, AX_X, ALU.max))
            tt(sc, sc, by_head(MX, N), ALU.subtract).then_inc(shifted, 1)

            for h in range(2):
                dve.wait_ge(relu_q_ready, h + 1)
                cols = slice(h * HALF, (h + 1) * HALF)
                ts(neg_q[0:N, cols], bank[BANKS["mq"] + h][0:N, :], 0.0, None, ALU.min)\
                    .then_inc(half_out, 1)
            dve.wait_ge(exps_ready, 1)
            link(nc.vector.tensor_reduce(head[0:N, SUM, :], sc, AX_X, ALU.add))
            link(nc.vector.reciprocal(head[0:N, INV, :], head[0:N, SUM, :]))
            tt(sc, sc, by_head(INV, N), ALU.mult).then_inc(attn_ready, 1)

            pr = prod[0:N, :].rearrange("n (h f) -> n h f", h=H)
            dve.wait_ge(half_out, AT["mq", 1] + 1)
            for h in range(2):
                dve.wait_ge(half_done, AT["mk", h] + 1)
                heads = slice(h * H // 2, (h + 1) * H // 2)
                cols = slice(h * HALF, (h + 1) * HALF)
                k_ps = bank[BANKS["mk"] + h][0:N, :].rearrange("n (h f) -> n h f", f=DH)
                stt(pr[:, heads, ROLL:ROLL + DH], k_ps, 0.0,
                    relu_q[0:N, cols].rearrange("n (h f) -> n h f", f=DH), ALU.max, ALU.mult)
                ins = stt(pr[:, heads, ROLL + DH:ROLL + FEAT], k_ps, 0.0,
                          neg_q[0:N, cols].rearrange("n (h f) -> n h f", f=DH), ALU.min, ALU.mult)
                ins.then_inc(half_out, 1)
            dve.wait_ge(half_out, AT["mk", 1] + 1)
            nc.vector.tensor_copy(pr[:, :, 0:ROLL], pr[:, :, FEAT:FEAT + ROLL]).then_inc(prod_ready, 1)
            dve.wait_ge(prod_ready, 1)
            ro = rolled[0:N, :].rearrange("n (h f) -> n h f", h=H)
            link(tt(ro, pr[:, :, 2:2 + FEAT], pr[:, :, 1:1 + FEAT], ALU.add))
            link(tt(ro, ro, pr[:, :, 0:FEAT], ALU.add))
            link(tt(ro, ro, pr[:, :, ROLL:ROLL + FEAT], ALU.mult))
            S, DEN, RDEN = 3, 4, 5
            link(nc.vector.tensor_reduce(head[0:N, S, :], ro, AX_X, ALU.add))
            link(ts(head[0:N, DEN, :], head[0:N, S, :], SCALE, EPS, ALU.mult, ALU.add))
            link(nc.vector.reciprocal(head[0:N, RDEN, :], head[0:N, DEN, :]))
            link(stt(head[0:N, S, :], head[0:N, S, :], SCALE, head[0:N, RDEN, :],
                     ALU.mult, ALU.mult))
            for h in range(2):
                dve.wait_ge(half_done, AT["mv", h] + 1)
                heads = slice(h * H // 2, (h + 1) * H // 2)
                cols = slice(h * HALF, (h + 1) * HALF)
                tt(mvec[0:N, cols].rearrange("n (h f) -> n h f", f=DH),
                   bank[BANKS["mv"] + h][0:N, :].rearrange("n (h f) -> n h f", f=DH),
                   by_head(S, DH)[:, heads, :], ALU.mult).then_inc(half_out, 1)

            dve.wait_ge(spread, 4)
            link(tt(xs[0:N, 0:D], xs[0:N, 0:D], beta[0:N, :], ALU.add))
            link(tt(xs[0:N, 0:D], xs[0:N, 0:D], bias_o_b[0:N, :], ALU.add))
            for h in range(2):
                dve.wait_ge(half_done, AT["mo", h] + 1)
                cols = slice(h * HALF, (h + 1) * HALF)
                ins = tt(acc[0:N, cols], bank[BANKS["mo"] + h][0:N, :], xn[0:N, cols], ALU.add)
                link(ins)
            layernorm_stats(acc, 32, varm_ready)
            dve.wait_ge(stdm_ready, 1)
            link(nc.vector.reciprocal(small[0:N, 36:37], small[0:N, 35:36]))
            for h in range(2):
                cols = slice(h * HALF, (h + 1) * HALF)
                link(stt(acc[0:N, cols], acc[0:N, cols], small[0:N, 32:33], gamma[0:N, cols],
                         ALU.subtract, ALU.mult))
                ins = stt(acc[0:N, cols], acc[0:N, cols], small[0:N, 36:37], xs[0:N, cols],
                          ALU.mult, ALU.add)
                if h == 0:
                    link(ins)
            ins.then_inc(pre_ready, 1)
            dve.wait_ge(pre_ready, 1)
            for h in range(2):
                dve.wait_ge(half_done, AT["wo", h] + 1)
                cols = slice(h * HALF, (h + 1) * HALF)
                link(tt(acc[0:N, cols], bank[BANKS["wo"] + h][0:N, :], acc[0:N, cols], ALU.add))
            layernorm_stats(acc, 40, var2_ready)
            dve.wait_ge(std2_ready, 1)
            link(nc.vector.reciprocal(small[0:N, 44:45], small[0:N, 43:44]))
            for h in range(2):
                ts(xn[0:N, h * HALF:(h + 1) * HALF], acc[0:N, h * HALF:(h + 1) * HALF],
                   small[0:N, 40:41], small[0:N, 44:45], ALU.subtract, ALU.mult)\
                    .then_inc(xn2_ready, 1)

            E1, SG, BI, RANK, SEL, W = range(1, 7)
            dve.wait_ge(gate_exp, 1)
            link(ts(route[0:N, E1, :], route[0:N, 0, :], 1.0, None, ALU.add))
            link(nc.vector.reciprocal(route[0:N, SG, :], route[0:N, E1, :]))
            dve.wait_ge(gate_landed, 32)
            link(tt(route[0:N, BI, :], route[0:N, SG, :], ebias[0:N, :], ALU.add))
            others = route[0:N, BI, :].unsqueeze(1).broadcast_to([N, EXPERTS, EXPERTS])
            own = route[0:N, BI, :].unsqueeze(2).broadcast_to([N, EXPERTS, EXPERTS])
            gt = beat[0:N, 0, :].rearrange("n (e o) -> n e o", e=EXPERTS)
            eq = beat[0:N, 1, :].rearrange("n (e o) -> n e o", e=EXPERTS)
            tt(gt, others, own, ALU.is_gt)
            link(tt(eq, others, own, ALU.is_equal))
            link(tt(eq, eq, lower[0:N, :, :], ALU.mult))
            link(tt(gt, gt, eq, ALU.add))
            link(nc.vector.tensor_reduce(route[0:N, RANK, :], gt, AX_X, ALU.add))
            link(ts(route[0:N, SEL, :], route[0:N, RANK, :], 2.0, None, ALU.is_lt))
            tt(route[0:N, W, :], route[0:N, SG, :], route[0:N, SEL, :], ALU.mult)\
                .then_inc(route_ready, 1)

            def shared_square(j, done):
                t0, t1 = TILES[j]
                dve.wait_ge(relu_done, done)
                r = sh_relu[:, t0 * N:t1 * N]
                tt(sh_h[:, t0 * N:t1 * N], r, r, ALU.mult).then_inc(h_ready, 1)

            shared_square(0, 1)
            for b in range(2):
                dve.wait_ge(w_all_psum, b + 1)
                nc.vector.tensor_copy(w_all[:, 4 * b:4 * b + 4, :],
                                      tiles(bank[2 + b][:, 0:GROUP * N])).then_inc(w_all_ready, 1)
            dve.wait_ge(w_all_ready, 2)
            tt(tiles(xe[:]), tiles(xnt[:]), w_all[:, 0:1, :].broadcast_to([P, KT, N]),
               ALU.mult).then_inc(xe_ready, 1)

            def square(e, used):
                for j, (t0, t1) in enumerate(TILES):
                    dve.wait_ge(relu_done, up_before(e) + (j + 1))
                    if j == 0 and used is not None:
                        dve.wait_ge(down_done, used)
                    r = e_relu[:, t0 * N:t1 * N]
                    tt(e_h[:, t0 * N:t1 * N], r, r, ALU.mult).then_inc(h_ready, 1)

            def scale_tokens(e, used):
                dve.wait_ge(up_done, used)
                tt(tiles(xe[:]), tiles(xnt[:]),
                   w_all[:, bass.ds(e, 1), :].broadcast_to([P, KT, N]), ALU.mult)\
                    .then_inc(xe_ready, 1)

            def add(e, before):
                for h in range(2):
                    dve.wait_ge(out_taken, e * 2 + (h + 1))
                    if before is not None:
                        dve.wait_ge(added, before + h)
                    cols = slice(h * HALF, (h + 1) * HALF)
                    tt(acc[0:N, cols], rounded[0:N, cols], acc[0:N, cols], ALU.add)\
                        .then_inc(added, 1)

            dve.wait_ge(h_ready, 1)
            square(0, None)
            scale_tokens(1, up_before(1))
            add(0, None)
            square(1, PARTS)
            scale_tokens(2, up_before(1) + PARTS)
            add(1, 1)
            for j in (1, 2):
                shared_square(j, 2 * PARTS + j + 1)
            dve.wait_ge(down_done, 3 * PARTS)
            for h in range(2):
                dve.wait_ge(added, 3 + h)
                cols = slice(h * HALF, (h + 1) * HALF)
                tt(acc[0:N, cols], bank[h][0:N, :], acc[0:N, cols], ALU.add).then_inc(added, 1)
            dve.wait_ge(h_ready, 3 * PARTS)
            square(2, 2 * PARTS)
            with dve.Fori(3, EXPERTS) as e:
                scale_tokens(e, e * PARTS + PARTS)
                add(e - 1, e * 2 - 1)
                square(e, e * PARTS + PARTS)
            add(EXPERTS - 1, 2 * EXPERTS - 1)

        @block.tensor
        def _(pe):
            mm = nc.tensor.matmul
            def spread_keys(r):
                for g in range(GROUP):
                    c = r * GROUP + g
                    for end in range(2):
                        at = end * EC + c
                        ins = mm(bank[KEY_BANKS[r]][:, g * P:(g + 1) * P],
                                 pick[:, at:at + 1].broadcast_to([EC, P]),
                                 ends_r[:, end * P:(end + 1) * P], start=(end == 0),
                                 stop=(end == 1))
                ins.then_inc(key_psum, 1)

            pe.wait_ge(ends_ready, 3)
            for r in range(4):
                spread_keys(r)

            def transpose_rows(src, banks, ready, psum):
                for b in range(2):
                    pe.wait_ge(ready, b + 1)
                    for g in range(GROUP):
                        k = b * GROUP + g
                        ins = nc.tensor.transpose(bank[banks + b][:, g * N:(g + 1) * N],
                                                  src[0:N, k * P:(k + 1) * P], ident[0:N, 0:N])
                    ins.then_inc(psum, 1)

            pe.wait_ge(pool_step, 2)
            transpose_rows(xn, 4, xn_ready, xnt_psum)
            pe.wait_ge(xnt_ready, 2)

            def out_transposed(m, h, src):
                c = AT[m, h]
                if c:
                    half_landed(pe, c)
                for o in range(HT):
                    if c == 0 and o == 0:
                        pe.wait_ge(first_landed, 16)
                    if c == 0 and o == 2:
                        half_landed(pe, c)
                    for k in range(KT):
                        ins = mm(bank[BANKS[m] + h][:, o * N:(o + 1) * N],
                                 slots[c % SLOTS][:, k, o * P:(o + 1) * P], tiles(src)[:, k, :],
                                 start=(k == 0), stop=(k == KT - 1))
                ins.then_inc(half_done, 1)

            def out_rows(m, h, src):
                c = AT[m, h]
                half_landed(pe, c)
                for k in range(KT):
                    ins = mm(bank[BANKS[m] + h][0:N, :], tiles(src)[:, k, :],
                             slots[c % SLOTS][:, k, :], start=(k == 0), stop=(k == KT - 1))
                ins.then_inc(half_done, 1)

            for h in range(2):
                out_transposed("wq", h, xnt[:])
            for r in range(4, 6):
                pe.wait_ge(key_used, r - 3)
                spread_keys(r)
            pe.wait_ge(key_used, 4)
            for h in range(2):
                out_transposed("wk", h, xnt[:])
            for h in range(2):
                pe.wait_ge(half_out, AT["wq", h] + 1)
                out_transposed("wv", h, xnt[:])
            pe.wait_ge(onehot_ready, 1)
            for r in range(5):
                if r >= 4:
                    pe.wait_ge(code_used, r - 3)
                for c in range(5 * r, min(5 * r + 5, EC)):
                    ins = mm(bank[4 + r % 4][0:N, (c - 5 * r) * N:(c - 5 * r + 1) * N],
                             oh_src[:, c, :], oh_dst[:, c, :], start=True, stop=True)
                ins.then_inc(code_psum, 1)
            pe.wait_ge(half_out, AT["wq", 1] + 1)
            for h in range(2):
                pe.wait_ge(half_out, AT["wk", h] + 1)
                out_transposed("wiq", h, q1)
            pe.wait_ge(half_out, AT["wk", 1] + 1)
            for h in range(2):
                pe.wait_ge(half_out, AT["wv", h] + 1)
                out_transposed("wik", h, k1)
            pe.wait_ge(half_out, AT["wv", 1] + 1)
            for h in range(2):
                pe.wait_ge(half_out, AT["wiq", h] + 1)
                out_rows("wiv", h, v1)
            pe.wait_ge(half_out, AT["wik", 1] + 1)
            pe.wait_ge(code_used, 5)
            for b in range(2):
                for g in range(GROUP):
                    for odd in range(2):
                        half = slice(DH * odd, DH * (odd + 1))
                        ins = mm(bank[4 + 2 * odd + b][0:N, g * N:(g + 1) * N],
                                 tiles(q2)[half, b * GROUP + g, :],
                                 tiles(k2)[half, b * GROUP + g, :], start=True, stop=True)
                ins.then_inc(scores_psum, 1)
            for h in range(2):
                pe.wait_ge(half_out, AT["wik", h] + 1)
                out_rows("mq", h, xnt[:])
            for h in range(2):
                pe.wait_ge(half_out, AT["wiv", h] + 1)
                out_rows("mk", h, xnt[:])
            pe.wait_ge(attn_ready, 1)
            for b in range(4):
                for g in range(GROUP):
                    at = b * GROUP + g
                    ins = nc.tensor.transpose(bank[4 + b][0:N, g * N:(g + 1) * N],
                                              scores[0:N, at * N:(at + 1) * N], ident[0:N, 0:N])
                ins.then_inc(attn_t_psum, 1)
            pe.wait_ge(relu_q_ready, 2)
            for h in range(2):
                pe.wait_ge(half_out, AT["mq", h] + 1)
                out_rows("mv", h, xnt[:])
            pe.wait_ge(attn_t_ready, 4)
            pe.wait_ge(half_out, AT["wiv", 1] + 1)
            for b in range(2):
                for g in range(2 * GROUP):
                    hd = b * 2 * GROUP + g
                    p0 = DH * (hd % 2)
                    at = PAIR * (hd % 2) + hd // 2
                    ins = mm(bank[4 + b][p0:p0 + DH, (g // 2) * N:(g // 2 + 1) * N],
                             v2[0:N, hd * DH:(hd + 1) * DH], attn_t[0:N, at * N:(at + 1) * N],
                             start=True, stop=True)
                ins.then_inc(pv_psum, 1)
            for b in range(2):
                pe.wait_ge(half_out, AT["mv", b] + 1)
                for g in range(GROUP):
                    k = b * GROUP + g
                    ins = nc.tensor.transpose(bank[6 + b][:, g * N:(g + 1) * N],
                                              mvec[0:N, k * P:(k + 1) * P], ident[0:N, 0:N])
                ins.then_inc(mvec_t_psum, 1)
            pe.wait_ge(out_t_ready, 2)
            out_rows("wo", 0, out_t)
            pe.wait_ge(mvec_t_ready, 2)
            pe.wait_ge(half_out, AT["mk", 1] + 1)
            out_rows("mo", 0, mvec_t)
            out_rows("mo", 1, mvec_t)
            out_rows("wo", 1, out_t)

            pe.wait_ge(pre_ready, 1)
            transpose_rows(xn, 2, xn2_ready, xn2t_psum)
            pe.wait_ge(xn2t_ready, 2)
            pe.wait_ge(gate_landed, 32)
            for k in range(KT):
                ins = mm(bank[7][0:N, 0:EXPERTS], tiles(xnt[:])[:, k, :],
                         gate[:, k * EXPERTS:(k + 1) * EXPERTS], start=(k == 0), stop=(k == KT - 1))
            ins.then_inc(logits_psum, 1)
            def shared_up_chunk(j):
                t0, t1 = TILES[j]
                pe.wait_ge(shared_landed[j], 16)
                for t in range(t0, t1):
                    for k in range(KT):
                        ins = mm(bank[4 + j][:, (t - t0) * N:(t - t0 + 1) * N], sh_up_t[:, t, k, :],
                                 tiles(xnt[:])[:, k, :], start=(k == 0), stop=(k == KT - 1))
                ins.then_inc(up_done, 1)

            def expert(e, b, turn, free):
                up = stage[b][:, 0:TT * UNIT // 2].bitcast(BF16)\
                    .rearrange("p (t k j) -> p t k j", t=TT, k=KT)
                down = stage[b][:, TT * UNIT // 2:TT * UNIT].bitcast(BF16)
                up0 = up_before(e)
                pe.wait_ge(xe_ready, e + 1)
                for j, (t0, t1) in enumerate(TILES):
                    pe.wait_ge(stage_landed[b][j], turn * 16 + 16)
                    pe.wait_ge(relu_done, 1 if isinstance(e, int) and e == 0 else up0 + (j + 1 - PARTS))
                    for t in range(t0, t1):
                        for k in range(KT):
                            ins = mm(bank[4 + j][:, (t - t0) * N:(t - t0 + 1) * N], up[:, t, k, :],
                                     tiles(xe[:])[:, k, :], start=(k == 0), stop=(k == KT - 1))
                    ins.then_inc(up_done, 1)
                if free is not None:
                    pe.wait_ge(*free)
                for j, (t0, t1) in enumerate(TILES):
                    pe.wait_ge(stage_landed[b][PARTS + j], turn * 16 + 16)
                    pe.wait_ge(h_ready, up0 + (j + 1))
                    for h in range(2):
                        for t in range(t0, t1):
                            at = t * UNIT + h * HALF
                            ins = mm(bank[h][0:N, :], tiles(e_h)[:, t, :], down[:, at:at + HALF],
                                     start=(t == 0), stop=(t == TT - 1))
                        if h == 0 and j == PARTS - 1:
                            ins.then_inc(down_first, 1)
                    ins.then_inc(down_done, 1)

            shared_up_chunk(0)
            pe.wait_ge(route_ready, 1)
            for b in range(2):
                for g in range(GROUP):
                    e = b * GROUP + g
                    ins = mm(bank[2 + b][:, g * N:(g + 1) * N],
                             route[0:N, 6, e:e + 1].broadcast_to([N, P]), ident[0:N, 0:N],
                             start=True, stop=True)
                ins.then_inc(w_all_psum, 1)
            expert(0, 0, 0, None)
            expert(1, 1, 0, (out_taken, 2))
            for j in (1, 2):
                pe.wait_ge(relu_done, up_before(1) + j + 1)
                shared_up_chunk(j)
            pe.wait_ge(out_taken, 4)
            pe.wait_ge(h_ready, 3 * PARTS)
            for j, (t0, t1) in enumerate(SH_DN_TILES):
                pe.wait_ge(shared_landed[PARTS + j], 16)
                for t in range(t0, t1):
                    for h in range(2):
                        w = sh_dn[j][:, (t - t0) * UNIT + h * HALF:(t - t0) * UNIT + (h + 1) * HALF]
                        ins = mm(bank[h][0:N, :], tiles(sh_h)[:, t, :], w,
                                 start=(t == 0), stop=(t == TT - 1))
                ins.then_inc(down_done, 1)
            with pe.Fori(0, 2) as i:
                for n in range(3):
                    e = i * 3 + (2 + n)
                    expert(e, n, i + (n < 2), (added, e * 2 + 2) if n == 0 else (out_taken, e * 2))


def kernel(**inputs):
    import numpy as np
    import concourse.bacc as bacc
    from concourse import mybir as mb
    from concourse.bass_utils import run_bass_kernel_spmd

    def tiled_rows(w):
        return w.reshape(KT, P, 2, HALF).transpose(2, 1, 0, 3).reshape(2, P, SLOT)

    g = {k: np.asarray(v) for k, v in inputs.items()}
    wkv = g["L0_mix_Wkv"]
    mats = {
        "wq": g["L0_gnn_wq"].T, "wk": g["L0_gnn_wk"].T, "wv": g["L0_gnn_wv"].T,
        "wiq": g["L0_gnn_wiq"].T, "wik": g["L0_gnn_wik"].T, "wiv": g["L0_gnn_wiv"].T,
        "mq": g["L0_mix_Wq"], "mk": wkv[:, :D], "mv": wkv[:, D:],
        "mo": g["L0_mix_Wo"], "wo": g["L0_gnn_wo"].T,
    }
    arrays = {"x": g["x"]}
    for name, w in mats.items():
        arrays[f"mat_{name}"] = tiled_rows(w)
    arrays["bias_cols"] = np.stack([g[f"L0_gnn_{b}"].reshape(KT, P).T
                                    for b in ("bq", "bk", "bv", "biq", "bik")], axis=1)\
        .reshape(P, len(BIASES) * KT)
    arrays["bias_v"] = g["L0_gnn_biv"].reshape(1, D)
    arrays["bias_o"] = g["L0_gnn_bo"].reshape(1, D)
    arrays["ln_gamma"] = g["L0_mix_ln_gamma"].reshape(1, D)
    arrays["ln_beta"] = g["L0_mix_ln_beta"].reshape(1, D)
    arrays["edge_rows"] = np.stack([g[k].reshape(EC, P) for k in ("src", "dst")], axis=1)\
        .reshape(EC, 2 * P)
    arrays["edge_cols"] = np.stack([g[k].reshape(EC, P).T for k in ("src", "dst", "edge_type_5")],
                                   axis=1)
    arrays["edge_w"] = g["L0_gnn_edge_type_weights"].reshape(1, ETYPES)
    arrays["gate_w"] = g["L0_ffn_gate_w"].reshape(EXPERTS, KT, P).transpose(2, 1, 0).reshape(P, KT * EXPERTS)
    arrays["expert_bias"] = g["L0_ffn_expert_bias"].reshape(1, EXPERTS)
    arrays["shared_up"] = g["L0_ffn_shared_w_up"].reshape(TT, P, KT, P).transpose(3, 0, 2, 1)\
        .reshape(P, TT * UNIT)
    arrays["shared_down"] = g["L0_ffn_shared_w_down"].reshape(D, TT, P).transpose(2, 1, 0)\
        .reshape(P, TT * UNIT)
    arrays["expert_up"] = g["L0_ffn_w_up"].reshape(EXPERTS, TT, P, KT, P).transpose(0, 4, 1, 3, 2)\
        .reshape(EXPERTS, P, TT * UNIT)
    arrays["expert_down"] = g["L0_ffn_w_down"].reshape(EXPERTS, D, TT, P).transpose(0, 3, 2, 1)\
        .reshape(EXPERTS, P, TT * UNIT)
    arrays = {f"in_{k}": np.ascontiguousarray(v) for k, v in arrays.items()}

    nc = bacc.Bacc("TRN2", target_bir_lowering=False, num_devices=1)
    aps = {k[3:]: nc.dram_tensor(k, a.shape, mb.dt.from_np(a.dtype), kind="ExternalInput").ap()
           for k, a in arrays.items()}
    out = nc.dram_tensor("out", (N, D), mb.dt.float32, kind="ExternalOutput").ap()
    mat_aps = {k[4:]: aps.pop(k) for k in list(aps) if k.startswith("mat_")}
    gps_layer(nc, mats=mat_aps, out=out, **aps)
    r = run_bass_kernel_spmd(nc, [arrays], core_ids=[0])
    return r.results[0]["out"]
```
